# Optimizing a Trainium2 kernel written in Bass

```python
import numpy as np
import jax
import jax.numpy as jnp

def _softmax(x, axis=-1):
    return jax.nn.softmax(x, axis=axis)

def _gelu(x):
    return jax.nn.gelu(x, approximate=True)

def _silu(x):
    return jax.nn.silu(x)

def _sigmoid(x):
    return jax.nn.sigmoid(x)

def _layernorm(x, axis=-1, eps=1e-05):
    m = jnp.mean(x, axis=axis, keepdims=True)
    v = jnp.var(x, axis=axis, keepdims=True)
    return (x - m) / jnp.sqrt(v + eps)

def _scatter_add(tgt, idx, src, axis=0):
    return tgt.at[idx].add(src)

def _segment_sum(src, seg, n):
    return jax.ops.segment_sum(src, seg, n)
kernel_name = 'mk_gnn_ffn_d1_gnn_r8_5db0a1'

def setup_inputs(seed: int=0):
    np.random.seed(seed)
    _w = jnp.asarray

    def _rec_inputs():
        import jax
        import jax.numpy as jnp
        _gk = jax.random.key(seed)
        x = -0.0002117 + 1 * jax.random.normal(jax.random.fold_in(_gk, 1), (6250, 512), jnp.float32)
        src = jax.random.randint(jax.random.fold_in(_gk, 2), (100000,), 0, 6250, jnp.int32)
        dst = jax.random.randint(jax.random.fold_in(_gk, 3), (100000,), 0, 6250, jnp.int32)
        _o = jnp.argsort(dst, stable=True)
        src = src[_o]
        dst = dst[_o]
        return (x, src, dst)
    x, src, dst = _rec_inputs()

    def _L0_gnn_setup():
        import jax, jax.numpy as jnp
        import numpy as np
        N_NODES = 6250
        D_IN = 512
        D_OUT = 512
        N_EDGES = 100000
        key = jax.random.key(seed)
        kx, ke, k1, k2, k3, k4 = jax.random.split(key, 6)
        x = jax.random.normal(kx, (N_NODES, D_IN), dtype=jnp.float32)
        edge_index = jax.random.randint(ke, (2, N_EDGES), 0, N_NODES, dtype=jnp.int64)
        b1lim = 1.0 / np.sqrt(D_IN)
        b2lim = 1.0 / np.sqrt(D_OUT)
        W1 = jax.random.uniform(k1, (D_IN, D_OUT), jnp.float32, -b1lim, b1lim)
        b1 = jax.random.uniform(k2, (D_OUT,), jnp.float32, -b1lim, b1lim)
        W2 = jax.random.uniform(k3, (D_OUT, D_OUT), jnp.float32, -b2lim, b2lim)
        b2 = jax.random.uniform(k4, (D_OUT,), jnp.float32, -b2lim, b2lim)
        return {'x': x, 'edge_index': edge_index, 'W1': W1, 'b1': b1, 'W2': W2, 'b2': b2}
    _L0_gnn_all = _L0_gnn_setup()
    _L0_gnn_in = {k: v for k, v in _L0_gnn_all.items() if k in ('W1', 'b1', 'W2', 'b2')}
    del _L0_gnn_all

    def _L0_ffn_setup():
        import jax, jax.numpy as jnp
        import numpy as np
        INPUT_SIZE = 512
        HIDDEN_SIZE = 512
        key = jax.random.key(seed)
        ks = jax.random.split(key, 9)
        B, T, I, H = (64, 512, INPUT_SIZE, HIDDEN_SIZE)
        scale = 1.0 / np.sqrt(I + H)
        x = jax.random.normal(ks[0], (B, T, I), dtype=jnp.float32)

        def lin(kw, kb):
            W = jax.random.uniform(kw, (I + H, H), minval=-scale, maxval=scale, dtype=jnp.float32)
            b = jax.random.uniform(kb, (H,), minval=-scale, maxval=scale, dtype=jnp.float32)
            return (W, b)
        W_f, b_f = lin(ks[1], ks[2])
        W_i, b_i = lin(ks[3], ks[4])
        W_c, b_c = lin(ks[5], ks[6])
        W_o, b_o = lin(ks[7], ks[8])
        return {'x': x, 'W_f': W_f, 'b_f': b_f, 'W_i': W_i, 'b_i': b_i, 'W_c': W_c, 'b_c': b_c, 'W_o': W_o, 'b_o': b_o}
    _L0_ffn_all = _L0_ffn_setup()
    _L0_ffn_in = {k: v for k, v in _L0_ffn_all.items() if k in ('W_f', 'b_f', 'W_i', 'b_i', 'W_c', 'b_c', 'W_o', 'b_o')}
    del _L0_ffn_all
    return {'x': x, 'src': src, 'dst': dst, 'L0_gnn_W1': _L0_gnn_in['W1'], 'L0_gnn_b1': _L0_gnn_in['b1'], 'L0_gnn_W2': _L0_gnn_in['W2'], 'L0_gnn_b2': _L0_gnn_in['b2'], 'L0_ffn_W_f': _L0_ffn_in['W_f'], 'L0_ffn_b_f': _L0_ffn_in['b_f'], 'L0_ffn_W_i': _L0_ffn_in['W_i'], 'L0_ffn_b_i': _L0_ffn_in['b_i'], 'L0_ffn_W_c': _L0_ffn_in['W_c'], 'L0_ffn_b_c': _L0_ffn_in['b_c'], 'L0_ffn_W_o': _L0_ffn_in['W_o'], 'L0_ffn_b_o': _L0_ffn_in['b_o']}

def reference(x, src, dst, L0_gnn_W1, L0_gnn_b1, L0_gnn_W2, L0_gnn_b2, L0_ffn_W_f, L0_ffn_b_f, L0_ffn_W_i, L0_ffn_b_i, L0_ffn_W_c, L0_ffn_b_c, L0_ffn_W_o, L0_ffn_b_o):
    import jax
    import jax.numpy as jnp

    def _L0_gnn_ref(x, edge_index, W1, b1, W2, b2):
        import jax, jax.numpy as jnp
        import numpy as np
        N_NODES = 6250
        D_IN = 512
        D_OUT = 512
        N_EDGES = 100000
        src, dst = (edge_index[0], edge_index[1])
        agg = jax.ops.segment_sum(x[src], dst, num_segments=N_NODES)
        h = x + agg
        h = jax.nn.relu(h @ W1 + b1)
        h = h @ W2 + b2
        return jax.nn.relu(h)

    def _L0_ffn_ref(x, W_f, b_f, W_i, b_i, W_c, b_c, W_o, b_o):
        import jax, jax.numpy as jnp
        import numpy as np
        INPUT_SIZE = 512
        HIDDEN_SIZE = 512
        B, T, I = x.shape
        H = W_f.shape[1]
        h0 = jnp.zeros((B, H), dtype=x.dtype)
        c0 = jnp.zeros((B, H), dtype=x.dtype)

        def step(carry, x_t):
            h_prev, c_prev = carry
            combined = jnp.concatenate((x_t, h_prev), axis=1)
            f_t = jax.nn.sigmoid(combined @ W_f + b_f)
            i_t = jax.nn.sigmoid(combined @ W_i + b_i)
            c_tilde = jnp.tanh(combined @ W_c + b_c)
            c_t = f_t * c_prev + i_t * c_tilde
            o_t = jax.nn.sigmoid(combined @ W_o + b_o)
            h_t = o_t * jnp.tanh(c_t)
            return ((h_t, c_t), h_t)
        _, hs = jax.lax.scan(step, (h0, c0), jnp.swapaxes(x, 0, 1))
        return jnp.swapaxes(hs, 0, 1)
    edge_index = jnp.stack([src, dst])
    x = x + _L0_gnn_ref(_layernorm(x, axis=-1), edge_index, L0_gnn_W1, L0_gnn_b1, L0_gnn_W2, L0_gnn_b2)
    x = x + _L0_ffn_ref(_layernorm(x, axis=-1)[None], L0_ffn_W_f, L0_ffn_b_f, L0_ffn_W_i, L0_ffn_b_i, L0_ffn_W_c, L0_ffn_b_c, L0_ffn_W_o, L0_ffn_b_o)[0]
    return x

_drawn_inputs = setup_inputs


def setup_inputs(seed=0):
    import zlib

    import numpy as np

    out = dict(_drawn_inputs(seed))
    spreads = {}
    factors = {'L0_gnn_b1': 8.0,
     'L0_gnn_b2': 3.732,
     'L0_ffn_W_f': 5.509,
     'L0_ffn_b_f': 64.0,
     'L0_ffn_W_i': 3.592,
     'L0_ffn_b_i': 64.0,
     'L0_ffn_b_c': 8.0,
     'L0_ffn_W_o': 3.281,
     'L0_ffn_b_o': 64.0}
    for name, (base, spread) in spreads.items():
        noise = np.random.default_rng([zlib.crc32(name.encode()), seed]).standard_normal(out[name].shape)
        drawn = base * np.exp(spread * noise) if base else spread * noise
        out[name] = jnp.asarray(drawn.astype(out[name].dtype))
    for name, factor in factors.items():
        out[name] = (out[name] * factor).astype(out[name].dtype)
    return out
```

```python
from contextlib import ExitStack

import concourse.bass as bass
from concourse import mybir

F32 = mybir.dt.float32
F32R = mybir.dt.float32r
BF16 = mybir.dt.bfloat16
I32 = mybir.dt.int32
ALU = mybir.AluOpType
ACT = mybir.ActivationFunctionType
AX_X = mybir.AxisListType.X

P = 128
EPS = 1e-5
LANES = 125
UNROLL = 4
LOAD_BLOCKS = 5
ROUGH = 3
FINE = 2
TOLERANCE = 2.0 ** -17


def program(nc, x, src, dst, W1, b1, W2, b2, Wg, bg, y):
    N, D = x.shape
    E, = src.shape
    K = D // P
    BLOCKS = N // LANES
    TILES = E // LANES
    STEPS = N // LANES
    G4 = 4 * D
    HALF = D // 2
    KH = K // 2
    PAIR = 2 * HALF
    assert N == BLOCKS * LANES and E == TILES * LANES and STEPS % 2 == 0 and PAIR == 512
    TPP = 8
    TROWS = TILES // TPP
    assert TROWS * TPP == TILES and TROWS <= P and BLOCKS <= P
    MORE = 2 * LANES

    table = nc.dram_tensor("ln_table", (N, D), F32, kind="Internal").ap()
    x1_rows = nc.dram_tensor("x1_rows", (N, D), F32, kind="Internal").ap()
    gate_rows = nc.dram_tensor("gate_rows", (N, G4), F32, kind="Internal").ap()

    with ExitStack() as top:
        def sb(stack, name, shape, dt=F32):
            return stack.enter_context(nc.sbuf_tensor(name, shape, dt))

        def pb(stack, name, shape, dt=F32):
            return stack.enter_context(nc.psum_tensor(name, shape, dt))

        def sem(stack, name):
            return stack.enter_context(nc.semaphore(name))

        ident = sb(top, "ident", [P, P])
        Wh = sb(top, "Wh", [P, K, 2, 2, 2, HALF])
        s_wh = sem(top, "s_wh")

        def gate_columns(w_sb, first_row):
            for half in range(2):
                for n, (bank, slot) in enumerate(((0, 0), (0, 1), (1, 0), (1, 1))):
                    yield (w_sb[:, :, half, bank, slot, :],
                           Wg[n][first_row:first_row + D, half * HALF:(half + 1) * HALF]
                           .rearrange("(k p) c -> p k c", p=P))

        WH_LOADS = 8

        with ExitStack() as first:
            src_cols = sb(first, "src_cols", [P, TILES + UNROLL], I32)
            dst_cols = sb(first, "dst_cols", [P, TILES + UNROLL])
            lo_row = sb(first, "lo_row", [1, BLOCKS], I32)
            ng_row = sb(first, "ng_row", [1, BLOCKS], I32)
            before_row = sb(first, "before_row", [1, BLOCKS], I32)

            table_part(nc, x, src, dst, table, ident, src_cols, dst_cols, lo_row, ng_row, before_row,
                       sb, pb, sem, N, D, TILES, BLOCKS, TPP, TROWS)
            graph_part(nc, x, table, x1_rows, gate_rows, W1, b1, W2, b2, bg, Wh, s_wh, gate_columns,
                       ident, src_cols, dst_cols, lo_row, ng_row, before_row,
                       sb, pb, sem, D, K, BLOCKS, TILES, G4, HALF, PAIR)
        lstm_part(nc, x1_rows, gate_rows, y, Wh, s_wh, WH_LOADS, ident,
                  sb, pb, sem, D, K, KH, STEPS, G4, HALF, PAIR, MORE)


def hold(e, passed, sem, value):
    e.wait_ge(sem, value)
    e.sem_inc(passed, 1)


def rsqrt_on_vector(e, after_own, var, root, r, t, s_root, roots, s_ready):
    e.wait_ge(s_root, roots)
    after_own(e.reciprocal(r, root))
    after_own(e.tensor_tensor(t, r, r, ALU.mult))
    after_own(e.tensor_tensor(t, t, var, ALU.mult))
    after_own(e.tensor_scalar(t, t, -0.5, 1.5, ALU.mult, ALU.add))
    after_own(e.tensor_tensor(r, r, t, ALU.mult))


def table_part(nc, x, src, dst, table, ident, src_cols, dst_cols, lo_row, ng_row, before_row,
               sb, pb, sem, N, D, TILES, BLOCKS, TPP, TROWS):
    LB = LOAD_BLOCKS
    GROUPS = BLOCKS // LB
    assert GROUPS * LB == BLOCKS and GROUPS % 2 == 0
    x_v = x.rearrange("(g j p) d -> g p j d", j=LB, p=LANES)
    table_v = table.rearrange("(g j p) d -> g p j d", j=LB, p=LANES)
    ETILE = LANES
    QUAD = 4

    with ExitStack() as ctx:
        xin = sb(ctx, "xin", [P, 2, LB, D])
        xout = sb(ctx, "xout", [P, 2, LB, D])
        stats = sb(ctx, "stats", [P, LB, 6])
        mv = sb(ctx, "mv", [P, LB, 2])
        ve = sb(ctx, "ve", [P, LB])
        root = sb(ctx, "root", [P, LB])
        rs = sb(ctx, "rs", [P, LB])
        rt = sb(ctx, "rt", [P, LB])
        raw_i = sb(ctx, "raw_i", [TROWS, 2, TPP * ETILE], I32)
        raw_f = sb(ctx, "raw_f", [TROWS, 2, TPP * ETILE])
        tmin = sb(ctx, "tmin", [TROWS, TPP])
        tmax = sb(ctx, "tmax", [TROWS, TPP])
        tile_no = sb(ctx, "tile_no", [TROWS, TPP])
        tile_up = sb(ctx, "tile_up", [TROWS, TPP])
        block_at = sb(ctx, "block_at", [TROWS, BLOCKS])
        key = sb(ctx, "key", [TROWS, TPP, BLOCKS])
        keys = sb(ctx, "keys", [TROWS, 2, TPP, BLOCKS])
        far = sb(ctx, "far", [TROWS, 2, BLOCKS])
        ends = sb(ctx, "ends", [BLOCKS, 2])
        row = sb(ctx, "row", [1, 8, BLOCKS])
        ones_row = sb(ctx, "ones_row", [1, BLOCKS])
        groups_i = sb(ctx, "groups_i", [1, BLOCKS], I32)
        turned = [pb(ctx, f"turned{n}", [P, QUAD, TROWS]) for n in range(4)]
        far_t = pb(ctx, "far_t", [BLOCKS, 2, TROWS])
        ends_t = pb(ctx, "ends_t", [1, 2, BLOCKS])

        s_x = [sem(ctx, f"s_x{n}") for n in range(2)]
        s_out = [sem(ctx, f"s_out{n}") for n in range(2)]
        s_raw = sem(ctx, "s_raw")
        s_ident = sem(ctx, "s_ident")
        s_ids = sem(ctx, "s_ids")
        s_own = sem(ctx, "s_own")
        s_var = sem(ctx, "s_var")
        s_root = sem(ctx, "s_root")
        s_norm = sem(ctx, "s_norm")
        s_float = sem(ctx, "s_float")
        s_turn = sem(ctx, "s_turn")
        s_far = sem(ctx, "s_far")
        s_far_t = sem(ctx, "s_far_t")
        s_ends = sem(ctx, "s_ends")
        s_ends_t = sem(ctx, "s_ends_t")

        block = ctx.enter_context(nc.Block())

        @block.sync
        def _(e):
            e.dma_start(raw_i[:, 0, :], src.rearrange("(p n) -> p n", p=TROWS)).then_inc(s_raw, 16)
            e.dma_start(raw_i[:, 1, :], dst.rearrange("(p n) -> p n", p=TROWS)).then_inc(s_raw, 16)
            for g in range(GROUPS):
                if g >= 2:
                    e.wait_ge(s_norm, g - 1)
                e.dma_start(xin[0:LANES, g % 2], x_v[g]).then_inc(s_x[g % 2], 16)
                if g >= 1:
                    e.wait_ge(s_norm, g)
                    e.dma_start(table_v[g - 1], xout[0:LANES, (g - 1) % 2]).then_inc(s_out[(g - 1) % 2], 16)
            e.wait_ge(s_norm, GROUPS)
            e.dma_start(table_v[GROUPS - 1], xout[0:LANES, (GROUPS - 1) % 2]).then_inc(s_out[(GROUPS - 1) % 2], 16)
            for n in range(2):
                e.wait_ge(s_out[n], 16 * (GROUPS // 2))

        @block.gpsimd
        def _(e):
            e.memset(ident[:, :], 0.0).then_inc(s_ident, 1)
            e.wait_ge(s_ident, 1)
            e.affine_select(out=ident[:, :], in_=ident[:, :], compare_op=ALU.not_equal, fill=1.0,
                            base=0, pattern=[[-1, P]], channel_multiplier=1).then_inc(s_ident, 1)
            e.memset(src_cols[:, TILES:], 0).then_inc(s_ids, 1)
            e.memset(dst_cols[:, TILES:], -1.0).then_inc(s_ids, 1)
            e.iota(block_at[:, :], pattern=[[LANES, BLOCKS]], base=0, channel_multiplier=0,
                   allow_small_or_imprecise_dtypes=True).then_inc(s_ids, 1)
            e.iota(tile_no[:, :], pattern=[[1, TPP]], base=1, channel_multiplier=TPP,
                   allow_small_or_imprecise_dtypes=True).then_inc(s_ids, 1)

        @block.scalar
        def _(e):
            for g in range(GROUPS):
                e.wait_ge(s_var, g + 1)
                e.activation(root[0:LANES, :], ve[0:LANES, :], ACT.Sqrt).then_inc(s_root, 1)

        @block.tensor
        def _(e):
            e.wait_ge(s_ident, 2)
            e.wait_ge(s_float, 1)
            for which in range(2):
                for j in range(TPP):
                    t = e.transpose(turned[2 * which + j // QUAD][0:ETILE, j % QUAD, :],
                                    raw_f[:, which, j * ETILE:(j + 1) * ETILE], ident[0:TROWS, 0:TROWS])
            t.then_inc(s_turn, 1)
            e.wait_ge(s_far, 1)
            for n in range(2):
                t = e.transpose(far_t[:, n, :], far[:, n, :], ident[0:TROWS, 0:TROWS])
            t.then_inc(s_far_t, 1)
            e.wait_ge(s_ends, 1)
            for n in range(2):
                t = e.transpose(ends_t[:, n, :], ends[:, n:n + 1], ident[0:BLOCKS, 0:BLOCKS])
            t.then_inc(s_ends_t, 1)

        @block.vector
        def _(e):
            own = [0]

            def after_own(ins):
                own[0] += 1
                ins.then_inc(s_own, 1)
                e.wait_ge(s_own, own[0])

            e.wait_ge(s_raw, 32)
            e.tensor_copy(raw_f[:, :, :], raw_i[:, :, :]).then_inc(s_float, 1)
            e.wait_ge(s_float, 1)
            dst_tiles = raw_f[:, 1, :].rearrange("p (j n) -> p j n", j=TPP)
            after_own(e.tensor_reduce(tmin[:, :], dst_tiles, AX_X, ALU.min))
            after_own(e.tensor_reduce(tmax[:, :], dst_tiles, AX_X, ALU.max))
            e.wait_ge(s_turn, 1)
            for which, cols in ((0, src_cols), (1, dst_cols)):
                by_tile = cols[0:ETILE, 0:TILES].rearrange("e (p j) -> e j p", j=TPP)
                for q in range(TPP // QUAD):
                    after_own(e.tensor_copy(by_tile[:, q * QUAD:(q + 1) * QUAD, :],
                                            turned[2 * which + q][0:ETILE, :, :]))

            e.wait_ge(s_ids, 4)
            after_own(e.tensor_scalar(tile_up[:, :], tile_no[:, :], -1.0, float(TILES + 1), ALU.mult, ALU.add))
            after_own(e.tensor_scalar(tmin[:, :], tmin[:, :], float(LANES), None, ALU.subtract))
            for n, number in enumerate((tile_no, tile_up)):
                for j in range(TPP):
                    after_own(e.tensor_scalar(key[:, j, :], block_at[:, :], tmin[:, j:j + 1],
                                              number[:, j:j + 1], ALU.is_gt, ALU.mult))
                    after_own(e.scalar_tensor_tensor(out=keys[:, n, j, :], in0=block_at[:, :],
                                                     scalar=tmax[:, j:j + 1], in1=key[:, j, :],
                                                     op0=ALU.is_le, op1=ALU.mult))
                r = e.tensor_reduce(far[:, n, :], keys[:, n].rearrange("p j b -> p b j"), AX_X, ALU.max)
                if n == 0:
                    after_own(r)
            r.then_inc(s_far, 1)
            e.wait_ge(s_far_t, 1)
            e.tensor_reduce(ends[:, :], far_t[:, :, :], AX_X, ALU.max).then_inc(s_ends, 1)
            e.wait_ge(s_ends_t, 1)
            after_own(e.tensor_copy(row[:, 0:2, :], ends_t[:, :, :]))
            end, low, count = row[:, 0, :], row[:, 2, :], row[:, 3, :]
            after_own(e.tensor_scalar(low, row[:, 1, :], -1.0, float(TILES), ALU.mult, ALU.add))
            after_own(e.tensor_tensor(count, end, low, ALU.subtract))
            after_own(e.tensor_scalar(count, count, float(UNROLL - 1), float(UNROLL), ALU.add, ALU.max))
            after_own(e.tensor_copy(groups_i[:, :], count))
            after_own(e.tensor_single_scalar(ng_row[:, :], groups_i[:, :], UNROLL.bit_length() - 1,
                                             ALU.arith_shift_right))
            groups, upto = row[:, 4, :], row[:, 5, :]
            after_own(e.tensor_copy(groups, ng_row[:, :]))
            after_own(e.memset(ones_row[:, :], 1.0))
            after_own(e.tensor_tensor_scan(upto, groups, ones_row[:, :], 0.0, ALU.add, ALU.mult))
            after_own(e.tensor_tensor(row[:, 6, :], upto, groups, ALU.subtract))
            after_own(e.tensor_copy(before_row[:, :], row[:, 6, :]))
            after_own(e.tensor_copy(lo_row[:, :], low))

            for g in range(GROUPS):
                b = g % 2
                e.wait_ge(s_x[b], 16 * (g // 2 + 1))
                for j in range(LB):
                    e.bn_stats(stats[0:LANES, j, :], xin[0:LANES, b, j, :]).then_inc(s_own, 1)
                own[0] += LB
                e.wait_ge(s_own, own[0])
                for j in range(LB):
                    e.bn_aggr(mv[0:LANES, j, :], stats[0:LANES, j, :]).then_inc(s_own, 1)
                own[0] += LB
                e.wait_ge(s_own, own[0])
                e.tensor_scalar_add(ve[0:LANES, :], mv[0:LANES, :, 1], EPS).then_inc(s_var, 1)
                e.wait_ge(s_var, g + 1)
                rsqrt_on_vector(e, after_own, ve[0:LANES, :], root[0:LANES, :], rs[0:LANES, :],
                                rt[0:LANES, :], s_root, g + 1, None)
                if g >= 2:
                    e.wait_ge(s_out[b], 16 * (g // 2))
                for j in range(LB):
                    n = e.tensor_scalar(xout[0:LANES, b, j, :], xin[0:LANES, b, j, :], mv[0:LANES, j, 0:1],
                                        rs[0:LANES, j:j + 1], ALU.subtract, ALU.mult)
                    if j < LB - 1:
                        after_own(n)
                n.then_inc(s_norm, 1)
                e.wait_ge(s_norm, g + 1)


def graph_part(nc, x, table, x1_rows, gate_rows, W1, b1, W2, b2, bg, Wh, s_wh, gate_columns,
               ident, src_cols, dst_cols, lo_row, ng_row, before_row,
               sb, pb, sem, D, K, BLOCKS, TILES, G4, HALF, PAIR):
    x_v = x.rearrange("(b p) d -> b p d", p=LANES)
    table_v = table.rearrange("(b p) d -> b p d", p=LANES)
    x1_v = x1_rows.rearrange("(b p) d -> b p d", p=LANES)
    gate_v = gate_rows.rearrange("(b p) d -> b p d", p=LANES)
    L = LANES
    BANKS = G4 // PAIR

    with ExitStack() as ctx:
        Wx = sb(ctx, "Wx", [P, K, 2, 2, 2, HALF])
        W1s = sb(ctx, "W1s", [P, K, D])
        W2s = sb(ctx, "W2s", [P, K, D])
        b1c = sb(ctx, "b1c", [P, K])
        b2r = sb(ctx, "b2r", [P, D])
        bgr = sb(ctx, "bgr", [P, BANKS, PAIR])
        zeros = sb(ctx, "zeros", [1, D], BF16)
        node_id = sb(ctx, "node_id", [P, L])
        idx = [sb(ctx, f"idx{j}", [P, 1], I32) for j in range(UNROLL)]
        rows = [sb(ctx, f"rows{j}", [P, D]) for j in range(UNROLL)]
        onehot = [sb(ctx, f"onehot{j}", [P, L]) for j in range(UNROLL)]
        xt = sb(ctx, "xt", [P, D])
        nt = sb(ctx, "nt", [P, D])
        hin = sb(ctx, "hin", [P, D])
        hinT = sb(ctx, "hinT", [P, K, L])
        h1T = sb(ctx, "h1T", [P, K, L])
        h2 = sb(ctx, "h2", [P, D])
        x1 = sb(ctx, "x1", [P, D])
        z = sb(ctx, "z", [P, D])
        zT = sb(ctx, "zT", [P, K, L])
        gout = sb(ctx, "gout", [P, 2, 2, PAIR])
        stats = sb(ctx, "gstats", [P, 6])
        mv = sb(ctx, "gmv", [P, 2])
        ve = sb(ctx, "gve", [P, 1])
        root = sb(ctx, "groot", [P, 1])
        rs = sb(ctx, "grs", [P, 1])
        rt = sb(ctx, "grt", [P, 1])
        agg = pb(ctx, "agg", [P, D])
        turned = pb(ctx, "rows_turned", [P, K, L])
        mid = [pb(ctx, f"mid{n}", [P, K // 2, L]) for n in range(2)]
        late = pb(ctx, "late", [P, D])
        gps = [pb(ctx, f"gps{n}", [P, PAIR]) for n in range(2)]

        s_w = sem(ctx, "s_w")
        s_xt = sem(ctx, "s_xt")
        s_nt = sem(ctx, "s_nt")
        s_zero = sem(ctx, "s_zero")
        s_rows = [sem(ctx, f"s_rows{j}") for j in range(UNROLL)]
        s_idx = sem(ctx, "s_idx")
        s_hot = sem(ctx, "s_hot")
        s_visit = sem(ctx, "s_visit")
        s_agg = sem(ctx, "s_agg")
        s_hin = sem(ctx, "s_hin")
        s_hin_t = sem(ctx, "s_hin_t")
        s_hinT = sem(ctx, "s_hinT")
        s_mid = [sem(ctx, f"s_mid{m}") for m in range(2)]
        s_h1 = [sem(ctx, f"s_h1{m}") for m in range(K)]
        s_late = sem(ctx, "s_late")
        s_own = sem(ctx, "s_gown")
        s_passed = sem(ctx, "s_gpassed")
        s_x1 = sem(ctx, "s_x1")
        s_var = sem(ctx, "s_gvar")
        s_root = sem(ctx, "s_groot")
        s_z = sem(ctx, "s_z")
        s_z_t = sem(ctx, "s_z_t")
        s_zT = sem(ctx, "s_zT")
        s_gps = [sem(ctx, f"s_gps{n}") for n in range(BANKS)]
        s_gout = [sem(ctx, f"s_gout{n}") for n in range(BANKS)]
        s_x1_st = sem(ctx, "s_x1_st")
        s_g_st = [sem(ctx, f"s_g_st{n}") for n in range(2)]

        WEIGHT_LOADS = 8 + 2 + 1 + 1 + 8
        block = ctx.enter_context(nc.Block())

        def block_range(e, b):
            many = e.value_load(ng_row[0:1, bass.ds(b, 1)], min_val=1, max_val=TILES // UNROLL)
            before = e.value_load(before_row[0:1, bass.ds(b, 1)], min_val=0, max_val=BLOCKS * TILES // UNROLL)
            return many, before

        def first_tile(e, b):
            return e.value_load(lo_row[0:1, bass.ds(b, 1)], min_val=0, max_val=TILES)

        def column(low, g, j):
            return nc.s_assert_within(
                low + g * UNROLL + j, 0, TILES + UNROLL - 1,
                skip_runtime_bounds_check_because="a range ends at TILES and is rounded up to UNROLL")

        @block.sync
        def _(e):
            with nc.allow_non_contiguous_dma(reason="small bias column"):
                e.dma_start(b1c[:, :], b1.rearrange("(m p) -> p m", p=P)).then_inc(s_w, 16)
            e.dma_start(b2r[:, :], b2.rearrange("(o d) -> o d", o=1).to_broadcast([P, D])).then_inc(s_w, 16)
            e.dma_start(W1s[:, :, :], W1.rearrange("(k p) c -> p k c", p=P)).then_inc(s_w, 16)
            e.dma_start(W2s[:, :, :], W2.rearrange("(k p) c -> p k c", p=P)).then_inc(s_w, 16)

            def load(b, first=False):
                if not first:
                    e.wait_ge(s_hin, b)
                e.dma_start(nt[0:L, :], table_v[b]).then_inc(s_nt, 16)
                if not first:
                    e.wait_ge(s_x1, b)
                e.dma_start(xt[0:L, :], x_v[b]).then_inc(s_xt, 16)

            def store_x1(b):
                e.wait_ge(s_x1, b + 1)
                e.dma_start(x1_v[b], x1[0:L, :]).then_inc(s_x1_st, 16)

            def store_gates(b):
                for half in range(2):
                    for n in range(2):
                        e.wait_ge(s_gout[2 * half + n], b + 1)
                    e.dma_start(gate_v[b][:, half * 2 * PAIR:(half + 1) * 2 * PAIR],
                                gout[0:L, half]).then_inc(s_g_st[half], 16)

            load(0, True)
            for dst_ap, src_ap in gate_columns(Wx, 0):
                e.dma_start(dst_ap, src_ap).then_inc(s_w, 16)
            for half in range(2):
                for n, (bank, slot) in enumerate(((0, 0), (0, 1), (1, 0), (1, 1))):
                    e.dma_start(bgr[:, 2 * half + bank, slot * HALF:(slot + 1) * HALF],
                                bg[n][half * HALF:(half + 1) * HALF].rearrange("(o d) -> o d", o=1)
                                .to_broadcast([P, HALF])).then_inc(s_w, 16)
            store_x1(0)
            for dst_ap, src_ap in gate_columns(Wh, D):
                e.dma_start(dst_ap, src_ap).then_inc(s_wh, 16)
            with e.Fori(1, BLOCKS) as b:
                load(b)
                store_gates(b - 1)
                store_x1(b)
            store_gates(BLOCKS - 1)
            e.wait_ge(s_x1_st, 16 * BLOCKS)
            for half in range(2):
                e.wait_ge(s_g_st[half], 16 * BLOCKS)

        @block.gpsimd
        def _(e):
            with e.Fori(0, BLOCKS) as b:
                many, before = block_range(e, b)
                low = first_tile(e, b)
                with e.Fori(0, many) as g:
                    for j in range(UNROLL):
                        visit = (before + g) * UNROLL + (j + 1)
                        e.wait_ge(s_visit, visit)
                        e.tensor_copy(idx[j][0:L, :], src_cols[0:L, bass.ds(column(low, g, j), 1)])\
                            .then_inc(s_idx, 1)
                        hold(e, s_passed, s_idx, visit)
                        e.indirect_dma_start(
                            out=rows[j][0:L, :], out_offset=None, in_=table[:, :],
                            in_offset=bass.IndirectOffsetOnAxis(ap=idx[j][0:L, 0:1], axis=0),
                        ).then_inc(s_rows[j], 16)

        @block.scalar
        def _(e):
            def turn_in(b):
                e.wait_ge(s_hin_t, b + 1)
                e.activation(hinT[:, :, :], turned[:, :, :], ACT.Copy).then_inc(s_hinT, 1)

            def turn_z(b):
                e.wait_ge(s_z_t, b + 1)
                e.activation(zT[:, :, :], turned[:, :, :], ACT.Copy).then_inc(s_zT, 1)

            def layers(b):
                turn_in(b)
                for m in range(K):
                    e.wait_ge(s_mid[m // 2], b + 1)
                    e.activation(h1T[:, m, :], mid[m // 2][:, m % 2, :], ACT.Relu, bias=b1c[:, m:m + 1]).then_inc(s_h1[m], 1)
                e.wait_ge(s_var, b + 1)
                e.activation(root[0:L, :], ve[0:L, :], ACT.Sqrt).then_inc(s_root, 1)

            e.wait_ge(s_w, 16 * WEIGHT_LOADS)
            layers(0)
            with e.Fori(1, BLOCKS) as b:
                turn_z(b - 1)
                layers(b)
            turn_z(BLOCKS - 1)

        @block.tensor
        def _(e):
            def visits(b):
                many, before = block_range(e, b)
                if not isinstance(b, int) or b > 0:
                    e.wait_ge(s_hin, b)
                e.matmul(agg[0:L, :], zeros[0:1, 0:L], zeros[0:1, :], start=True, stop=False,
                         skip_group_check=True)
                with e.Fori(0, many) as g:
                    q = before + g
                    for j in range(UNROLL):
                        e.wait_ge(s_rows[j], (q + 1) * 16)
                        e.wait_ge(s_hot, q * UNROLL + (j + 1))
                        e.matmul(agg[0:L, :], onehot[j][0:L, :], rows[j][0:L, :], start=False,
                                 stop=False, skip_group_check=True).then_inc(s_visit, 1)
                e.matmul(agg[0:L, :], zeros[0:1, 0:L], zeros[0:1, :], start=False, stop=True,
                         skip_group_check=True).then_inc(s_agg, 1)

            def turn_z(b):
                e.wait_ge(s_z, b + 1)
                for k in range(K):
                    t = e.transpose(turned[:, k, :], z[0:L, k * P:(k + 1) * P], ident[0:L, 0:L])
                t.then_inc(s_z_t, 1)
                e.wait_ge(s_zT, b + 1)

            def gates(b, half, first):
                for n in (2 * half, 2 * half + 1):
                    if n >= 2:
                        e.wait_ge(s_gout[n - 2], b + 1)
                    elif not first:
                        e.wait_ge(s_gout[n + 2], b)
                    for k in range(K):
                        m = e.matmul(gps[n % 2][0:L, :], zT[:, k, :],
                                     Wx[:, k, n // 2, n % 2].rearrange("p s c -> p (s c)"),
                                     start=(k == 0), stop=(k == K - 1))
                    m.then_inc(s_gps[n], 1)

            def layers(b):
                e.wait_ge(s_hin, b + 1)
                for k in range(K):
                    t = e.transpose(turned[:, k, :], hin[0:L, k * P:(k + 1) * P], ident[0:L, 0:L])
                t.then_inc(s_hin_t, 1)
                e.wait_ge(s_hinT, b + 1)
                for m in range(K):
                    for k in range(K):
                        mm = e.matmul(mid[m // 2][:, m % 2, :], W1s[:, k, m * P:(m + 1) * P], hinT[:, k, :],
                                      start=(k == 0), stop=(k == K - 1))
                    if m % 2:
                        mm.then_inc(s_mid[m // 2], 1)
                for k in range(K):
                    e.wait_ge(s_h1[k], b + 1)
                    mm = e.matmul(late[0:L, :], h1T[:, k, :], W2s[:, k, :], start=(k == 0), stop=(k == K - 1))
                mm.then_inc(s_late, 1)

            e.wait_ge(s_w, 16 * WEIGHT_LOADS)
            e.wait_ge(s_zero, 1)
            e.sem_inc(s_visit, UNROLL)
            visits(0)
            layers(0)
            with e.Fori(1, 2) as b:
                visits(b)
                turn_z(b - 1)
                gates(b - 1, 0, True)
                layers(b)
                gates(b - 1, 1, True)
            with e.Fori(2, BLOCKS) as b:
                visits(b)
                turn_z(b - 1)
                gates(b - 1, 0, False)
                layers(b)
                gates(b - 1, 1, False)
            turn_z(BLOCKS - 1)
            gates(BLOCKS - 1, 0, False)
            gates(BLOCKS - 1, 1, False)

        @block.vector
        def _(e):
            OWN = 12

            def one_hots(b):
                many, before = block_range(e, b)
                low = first_tile(e, b)
                with e.Fori(0, many) as g:
                    for j in range(UNROLL):
                        e.wait_ge(s_visit, (before + g) * UNROLL + (j + 1))
                        e.tensor_scalar(onehot[j][0:L, :], node_id[0:L, :],
                                        dst_cols[0:L, bass.ds(column(low, g, j), 1)], None,
                                        ALU.is_equal).then_inc(s_hot, 1)

            def gate_biases(b, half, first):
                if not first:
                    e.wait_ge(s_g_st[half], b * 16)
                for n in (2 * half, 2 * half + 1):
                    e.wait_ge(s_gps[n], b + 1)
                    e.tensor_tensor(gout[0:L, half, n % 2, :], gps[n % 2][0:L, :], bgr[0:L, n, :],
                                    ALU.add).then_inc(s_gout[n], 1)

            def add_own_rows(b):
                e.wait_ge(s_agg, b + 1)
                e.wait_ge(s_nt, (b + 1) * 16)
                if not isinstance(b, int) or b > 0:
                    e.wait_ge(s_hin_t, b)
                e.tensor_tensor(hin[0:L, :], agg[0:L, :], nt[0:L, :], ALU.add).then_inc(s_hin, 1)

            def out_and_norm(b):
                own = [b * OWN]

                def after_own(ins):
                    own[0] = own[0] + 1
                    ins.then_inc(s_own, 1)
                    e.wait_ge(s_own, own[0])

                after_own(e.tensor_scalar_add(node_id[0:L, :], node_id[0:L, :], float(L)))
                e.wait_ge(s_late, b + 1)
                after_own(e.tensor_tensor(h2[0:L, :], late[0:L, :], b2r[0:L, :], ALU.add))
                e.wait_ge(s_xt, (b + 1) * 16)
                if not isinstance(b, int) or b > 0:
                    e.wait_ge(s_x1_st, b * 16)
                e.scalar_tensor_tensor(out=x1[0:L, :], in0=h2[0:L, :], scalar=0.0, in1=xt[0:L, :],
                                       op0=ALU.max, op1=ALU.add).then_inc(s_x1, 1)
                e.wait_ge(s_x1, b + 1)
                e.bn_stats(stats[0:L, :], x1[0:L, :]).then_inc(s_own, 1)
                own[0] = own[0] + 1
                hold(e, s_passed, s_own, own[0])
                after_own(e.bn_aggr(mv[0:L, :], stats[0:L, :]))
                e.tensor_scalar_add(ve[0:L, :], mv[0:L, 1:2], EPS).then_inc(s_var, 1)
                e.wait_ge(s_var, b + 1)
                rsqrt_on_vector(e, after_own, ve[0:L, :], root[0:L, :], rs[0:L, :], rt[0:L, :],
                                s_root, b + 1, None)
                if not isinstance(b, int) or b > 0:
                    e.wait_ge(s_z_t, b)
                e.tensor_scalar(z[0:L, :], x1[0:L, :], mv[0:L, 0:1], rs[0:L, 0:1], ALU.subtract,
                                ALU.mult).then_inc(s_z, 1)
                e.sem_inc(s_own, OWN - (4 + 5))
                e.wait_ge(s_z, b + 1)

            e.memset(zeros[:, :], 0.0).then_inc(s_zero, 1)
            e.wait_ge(s_w, 16 * WEIGHT_LOADS)
            e.memset(node_id[0:L, :], 0.0).then_inc(s_zero, 1)
            e.memset(hin[0:L, 0:L], 1.0).then_inc(s_zero, 1)
            e.wait_ge(s_zero, 3)
            e.tensor_tensor_scan(node_id[0:L, :], hin[0:L, 0:L], hin[0:L, 0:L], -1.0, ALU.add,
                                 ALU.mult).then_inc(s_zero, 1)
            e.wait_ge(s_zero, 4)

            one_hots(0)
            add_own_rows(0)
            out_and_norm(0)
            with e.Fori(1, 2) as b:
                one_hots(b)
                add_own_rows(b)
                gate_biases(b - 1, 0, True)
                out_and_norm(b)
                gate_biases(b - 1, 1, True)
            with e.Fori(2, BLOCKS) as b:
                one_hots(b)
                add_own_rows(b)
                gate_biases(b - 1, 0, False)
                out_and_norm(b)
                gate_biases(b - 1, 1, False)
            gate_biases(BLOCKS - 1, 0, False)
            gate_biases(BLOCKS - 1, 1, False)


def lstm_part(nc, x1_rows, gate_rows, y, Wh, s_wh, WH_LOADS, ident,
              sb, pb, sem, D, K, KH, STEPS, G4, HALF, PAIR, MORE):
    L = LANES
    AHEAD = 2
    gates_v = gate_rows.rearrange("(c t) g -> t c g", t=STEPS)
    x1_v = x1_rows.rearrange("(c t) d -> t c d", t=STEPS)
    y_v = y.rearrange("(c t) d -> t c d", t=STEPS)

    with ExitStack() as ctx:
        Wr = sb(ctx, "Wr", [P, K, 2, 2, 2, HALF], F32R)
        hT = sb(ctx, "hT", [P, K, L])
        hTr = sb(ctx, "hTr", [P, K, L], F32R)
        xg = [sb(ctx, f"xg{n}", [P, 2, 2, PAIR]) for n in range(2)]
        total = sb(ctx, "total", [P, 2, 2, PAIR])
        gate = sb(ctx, "gate", [P, 2, 2, 2, HALF])
        c = sb(ctx, "c", [P, 2, HALF])
        fc = sb(ctx, "fc", [P, 2, HALF])
        ic = sb(ctx, "ic", [P, 2, HALF])
        tc = sb(ctx, "tc", [P, 2, HALF])
        h = [sb(ctx, f"h{n}", [P, 2, HALF]) for n in range(2)]
        decay = sb(ctx, "decay", [P, 2, HALF])
        x1 = [sb(ctx, f"lx1{n}", [P, D]) for n in range(2)]
        out = [sb(ctx, f"out{n}", [P, D]) for n in range(2)]
        c_start = sb(ctx, "c_start", [P, K, L])
        h_start = sb(ctx, "h_start", [P, K, L])
        gap = sb(ctx, "gap", [P, K, L])
        h_gap = sb(ctx, "h_gap", [P, K, L])
        change = sb(ctx, "change", [P, K, L])
        tc_start = sb(ctx, "tc_start", [P, K, L])
        most = sb(ctx, "most", [P, 4])
        worst = sb(ctx, "worst", [P, 1])
        worst1 = sb(ctx, "worst1", [1, 2])
        apart = sb(ctx, "apart", [1, 1], I32)

        acc = [pb(ctx, f"acc{n}", [P, PAIR]) for n in range(4)]
        hturn = [pb(ctx, f"hturn{n}", [P, KH, L]) for n in range(2)]
        back = pb(ctx, "back", [P, D])
        worst_t = pb(ctx, "worst_t", [1, P])
        c_end_t, decay_t, out_gate_t = (acc[n][:, 0:K * L].rearrange("p (k l) -> p k l", k=K) for n in range(3))

        s_acc = [sem(ctx, f"s_acc{n}") for n in range(4)]
        s_sum = [sem(ctx, f"s_sum{n}") for n in range(4)]
        s_fi = [sem(ctx, f"s_fi{n}") for n in range(2)]
        s_ct = [sem(ctx, f"s_ct{n}") for n in range(2)]
        s_o = [sem(ctx, f"s_o{n}") for n in range(2)]
        s_prod = [sem(ctx, f"s_prod{n}") for n in range(2)]
        s_c = [sem(ctx, f"s_c{n}") for n in range(2)]
        s_tc = [sem(ctx, f"s_tc{n}") for n in range(2)]
        s_h = [sem(ctx, f"s_h{n}") for n in range(2)]
        s_turn = [sem(ctx, f"s_lturn{n}") for n in range(2)]
        s_hT = [sem(ctx, f"s_hT{n}") for n in range(2)]
        s_decay = [sem(ctx, f"s_decay{n}") for n in range(2)]
        s_xg = [sem(ctx, f"s_xg{n}") for n in range(2)]
        s_x1 = [sem(ctx, f"s_lx1{n}") for n in range(2)]
        s_out = sem(ctx, "s_lout")
        s_y = [sem(ctx, f"s_y{n}") for n in range(2)]
        s_init = sem(ctx, "s_init")
        s_own = sem(ctx, "s_lown")
        s_ends = sem(ctx, "s_lends")
        s_cs = sem(ctx, "s_cs")
        s_tcs = sem(ctx, "s_tcs")
        s_back = sem(ctx, "s_back")
        s_begin = sem(ctx, "s_begin")
        s_fresh = sem(ctx, "s_fresh")
        s_worst = sem(ctx, "s_worst")
        s_worst_t = sem(ctx, "s_worst_t")
        s_apart = sem(ctx, "s_apart")
        s_passed = sem(ctx, "s_lpassed")

        block = ctx.enter_context(nc.Block())

        def steps_of_round(e, r, step):
            base = r * STEPS + AHEAD + 1
            step(0, 0, base, True, False)
            with e.Fori(0, STEPS // 2 - 1) as i:
                step(i * 2 + 1, 1, base + i * 2 + 1, False, False)
                step(i * 2 + 2, 0, base + i * 2 + 2, False, False)
            step(STEPS - 1, 1, base + (STEPS - 1), False, True)

        def all_rounds(e, one_round, signal_anyway=None):
            with e.Fori(0, ROUGH) as r:
                one_round(r, False, False, r)
            for f in range(FINE - 1):
                one_round(ROUGH + f, True, False, f)
            one_round(ROUGH + FINE - 1, True, True, FINE - 1)

            def not_met(checks):
                hold(e, s_passed, s_apart, checks)
                return e.value_load(apart[0:1, 0:1], min_val=0, max_val=1)

            with e.If(not_met(FINE) == 1):
                with e.Fori(0, MORE) as m:
                    with e.If(not_met(m + FINE) == 1):
                        one_round(m + (ROUGH + FINE), True, True, m + FINE)
                    with e.Else():
                        if signal_anyway is not None:
                            e.sem_inc(signal_anyway, 1)

        @block.sync
        def _(e):
            for n in range(2):
                e.sem_inc(s_y[n], 16)
            def one_round(r, fine, writes, checked):
                def step(s, par, now, first, last):
                    e.wait_ge(s_sum[3], now - 2)
                    e.dma_start(xg[par][0:L].rearrange("c a b g -> c (a b g)"), gates_v[s]).then_inc(s_xg[par], 16)
                    if writes:
                        e.wait_ge(s_out, now - 2)
                        e.dma_start(x1[par][0:L, :], x1_v[s]).then_inc(s_x1[par], 16)
                        e.wait_ge(s_out, now)
                        e.dma_start(y_v[s], out[par][0:L, :]).then_inc(s_y[par], 16)
                steps_of_round(e, r, step)
                if writes:
                    written = (r - (ROUGH + FINE - 1) + 1) * (STEPS // 2)
                    for n in range(2):
                        hold(e, s_passed, s_y[n], written * 16 + 16)
            all_rounds(e, one_round)

        @block.gpsimd
        def _(e):
            for s in s_decay:
                e.sem_inc(s, AHEAD)
            e.sem_inc(s_out, AHEAD + (ROUGH + FINE - 1) * STEPS)

            def one_round(r, fine, writes, checked):
                e.wait_ge(s_fresh, r + 1)
                def step(s, par, now, first, last):
                    for half in range(2):
                        e.wait_ge(s_fi[half], now)
                        e.wait_ge(s_decay[half], now - 1)
                        e.tensor_tensor(decay[0:L, half], decay[0:L, half], gate[0:L, half, 0, 0],
                                        ALU.mult).then_inc(s_decay[half], 1)
                    if writes:
                        n = now - (AHEAD + 1) - (ROUGH + FINE - 1) * STEPS
                        e.wait_ge(s_x1[par], (n - par) * 8 + 16)
                        e.wait_ge(s_y[par], (n - par) * 8 + 16)
                        for half in range(2):
                            e.wait_ge(s_h[half], now)
                        e.tensor_tensor(out[par][0:L, :], h[par][0:L].rearrange("c a u -> c (a u)"),
                                        x1[par][0:L, :], ALU.add).then_inc(s_out, 1)
                steps_of_round(e, r, step)
            all_rounds(e, one_round)

        @block.scalar
        def _(e):
            for s in (*s_fi, *s_ct, *s_o, *s_tc, *s_hT):
                e.sem_inc(s, AHEAD)
            e.wait_ge(s_wh, 16 * WH_LOADS)
            e.activation(Wr[:, 0:1, 0, 0, 0, 0:2], Wh[:, 0:1, 0, 0, 0, 0:2], ACT.Sigmoid).then_inc(s_init, 1)
            e.wait_ge(s_init, 1)
            for k in range(K):
                e.activation(Wr[:, k], Wh[:, k], ACT.Copy).then_inc(s_init, 1)

            def one_round(r, fine, writes, checked):
                turned = hT if fine else hTr

                def take_turned(half, now):
                    e.wait_ge(s_turn[half], now)
                    e.activation(turned[:, half * KH:(half + 1) * KH, :], hturn[half][:, :, :],
                                 ACT.Copy).then_inc(s_hT[half], 1)

                def step(s, par, now, first, last):
                    if not first:
                        take_turned(1, now - 1)
                    else:
                        e.wait_ge(s_begin, r + 1)
                    def forget_input(half):
                        e.wait_ge(s_sum[2 * half], now)
                        e.wait_ge(s_decay[half], now - 1)
                        e.activation(gate[0:L, half, 0].rearrange("c s u -> c (s u)"), total[0:L, half, 0],
                                     ACT.Sigmoid).then_inc(s_fi[half], 1)

                    def cell_output(half):
                        e.wait_ge(s_sum[2 * half + 1], now)
                        e.activation(gate[0:L, half, 1, 0], total[0:L, half, 1, 0:HALF],
                                     ACT.Tanh).then_inc(s_ct[half], 1)
                        e.activation(gate[0:L, half, 1, 1], total[0:L, half, 1, HALF:PAIR],
                                     ACT.Sigmoid).then_inc(s_o[half], 1)

                    def new_cell(half):
                        e.wait_ge(s_c[half], now)
                        e.activation(tc[0:L, half], c[0:L, half], ACT.Tanh).then_inc(s_tc[half], 1)

                    forget_input(0)
                    cell_output(0)
                    new_cell(0)
                    forget_input(1)
                    take_turned(0, now)
                    cell_output(1)
                    new_cell(1)
                    if last:
                        take_turned(1, now)
                steps_of_round(e, r, step)
                e.wait_ge(s_cs, r + 1)
                e.activation(tc_start[:, :, :], c_start[:, :, :], ACT.Tanh).then_inc(s_tcs, 1)
            all_rounds(e, one_round)

        @block.tensor
        def _(e):
            for s in (*s_acc, *s_turn):
                e.sem_inc(s, AHEAD)
            e.wait_ge(s_init, 1 + K)

            def one_round(r, fine, writes, checked):
                state, weights = (hT, Wh) if fine else (hTr, Wr)

                def products(n, ks):
                    for k in ks:
                        m = e.matmul(acc[n][0:L, :], state[:, k, :],
                                     weights[:, k, n // 2, n % 2].rearrange("p s c -> p (s c)"),
                                     start=(k == 0), stop=(k == K - 1), skip_group_check=True)
                    return m

                def turn(half, par, now):
                    e.wait_ge(s_h[half], now)
                    for k in range(KH):
                        t = e.transpose(hturn[half][:, k, :], h[par][0:L, half, k * P:(k + 1) * P],
                                        ident[0:L, 0:L])
                    t.then_inc(s_turn[half], 1)

                def step(s, par, now, first, last):
                    if first:
                        e.wait_ge(s_begin, r + 1)
                    else:
                        e.wait_ge(s_hT[0], now - 1)
                    for n in range(4):
                        e.wait_ge(s_sum[n], now - 1)
                        products(n, range(KH))
                    if not first:
                        turn(1, 1 - par, now - 1)
                        e.wait_ge(s_hT[1], now - 1)
                    for n in range(3):
                        products(n, range(KH, K)).then_inc(s_acc[n], 1)
                    products(3, range(KH, K - 1))
                    turn(0, par, now)
                    products(3, range(K - 1, K)).then_inc(s_acc[3], 1)
                    if last:
                        turn(1, par, now)
                steps_of_round(e, r, step)

                now = (r + 1) * STEPS + AHEAD
                for half in range(2):
                    e.wait_ge(s_c[half], now)
                    e.wait_ge(s_decay[half], now)
                    e.wait_ge(s_o[half], now)
                for n in range(4):
                    e.wait_ge(s_sum[n], now)
                for to, of in ((c_end_t, c), (decay_t, decay), (out_gate_t, gate[:, :, 1, 1])):
                    for k in range(K):
                        u = (k % KH) * P
                        t = e.transpose(to[:, k, :], of[0:L, k // KH, u:u + P], ident[0:L, 0:L])
                t.then_inc(s_ends, 1)
                if fine:
                    e.wait_ge(s_worst, checked + 1)
                    e.transpose(worst_t[:, :], worst[:, :], ident[:, :]).then_inc(s_worst_t, 1)
                e.wait_ge(s_cs, r + 1)
                for k in range(K):
                    t = e.transpose(back[0:L, k * P:(k + 1) * P], c_start[:, k, :], ident[:, :])
                t.then_inc(s_back, 1)
            all_rounds(e, one_round)

        @block.vector
        def _(e):
            for s in (*s_sum, *s_c, *s_h):
                e.sem_inc(s, AHEAD)
            for s in s_prod:
                e.sem_inc(s, 2 * AHEAD)
            clear = (c, hT, c_start, h_start, gap, h_gap, change)
            for t in clear:
                e.memset(t[:, :, :], 0.0).then_inc(s_own, 1)
            e.memset(decay[:, :, :], 1.0).then_inc(s_fresh, 1)
            e.wait_ge(s_own, len(clear))
            e.tensor_copy(hTr[:, :, :], hT[:, :, :]).then_inc(s_begin, 1)
            CLEARED = len(clear)
            ROUGH_OWN, FINE_OWN = 12, 22

            def one_round(r, fine, writes, checked):
                def step(s, par, now, first, last):
                    count = now - (AHEAD + 1)
                    def add_inputs(n):
                        half, bank = n // 2, n % 2
                        e.wait_ge(s_acc[n], now)
                        if n == 0:
                            e.wait_ge(s_xg[par], (count - par) * 8 + 16)
                        if bank == 0:
                            e.wait_ge(s_fi[half], now - 1)
                        else:
                            e.wait_ge(s_o[half], now - 1)
                        e.tensor_tensor(total[0:L, half, bank], acc[n][0:L, :], xg[par][0:L, half, bank],
                                        ALU.add).then_inc(s_sum[n], 1)

                    def new_cell(half):
                        e.wait_ge(s_fi[half], now)
                        e.tensor_tensor(fc[0:L, half], gate[0:L, half, 0, 0], c[0:L, half],
                                        ALU.mult).then_inc(s_prod[half], 1)
                        e.wait_ge(s_ct[half], now)
                        e.tensor_tensor(ic[0:L, half], gate[0:L, half, 0, 1], gate[0:L, half, 1, 0],
                                        ALU.mult).then_inc(s_prod[half], 1)
                        e.wait_ge(s_prod[half], now * 2)
                        e.tensor_tensor(c[0:L, half], fc[0:L, half], ic[0:L, half],
                                        ALU.add).then_inc(s_c[half], 1)

                    def new_h(half):
                        e.wait_ge(s_o[half], now)
                        e.wait_ge(s_tc[half], now)
                        if writes and half == 0:
                            e.wait_ge(s_out, now - 1)
                        e.tensor_tensor(h[par][0:L, half], gate[0:L, half, 1, 1], tc[0:L, half],
                                        ALU.mult).then_inc(s_h[half], 1)

                    add_inputs(0)
                    add_inputs(1)
                    new_cell(0)
                    add_inputs(2)
                    new_h(0)
                    add_inputs(3)
                    new_cell(1)
                    new_h(1)
                steps_of_round(e, r, step)

                own = [(r - ROUGH) * FINE_OWN + ROUGH * ROUGH_OWN + CLEARED if fine
                       else r * ROUGH_OWN + CLEARED]

                def after_own(ins):
                    own[0] = own[0] + 1
                    ins.then_inc(s_own, 1)
                    e.wait_ge(s_own, own[0])

                signals = 0
                e.wait_ge(s_ends, r + 1)
                after_own(e.tensor_tensor(gap[:, :, 1:], c_end_t[:, :, 0:L - 1], c_start[:, :, 1:], ALU.subtract))
                signals += 1
                if fine:
                    for half in range(2):
                        e.wait_ge(s_hT[half], (r + 1) * STEPS + AHEAD)
                    after_own(e.tensor_tensor(h_gap[:, :, 1:], hT[:, :, 0:L - 1], h_start[:, :, 1:],
                                              ALU.subtract))
                    for n, (g, op) in enumerate(((gap, ALU.max), (h_gap, ALU.max), (gap, ALU.min), (h_gap, ALU.min))):
                        after_own(e.tensor_reduce(most[:, n:n + 1], g[:, :, :].rearrange("p k l -> p (k l)"),
                                                  AX_X, op))
                    after_own(e.tensor_scalar(most[:, 2:4], most[:, 2:4], -1.0, None, ALU.mult))
                    e.tensor_reduce(worst[:, :], most[:, :], AX_X, ALU.max).then_inc(s_worst, 1)
                    e.wait_ge(s_worst_t, checked + 1)
                    after_own(e.tensor_reduce(worst1[:, 0:1], worst_t[:, :], AX_X, ALU.max))
                    after_own(e.tensor_scalar(worst1[:, 1:2], worst1[:, 0:1], TOLERANCE, None, ALU.is_gt))
                    e.tensor_copy(apart[:, :], worst1[:, 1:2]).then_inc(s_apart, 1)
                    signals += 1 + 4 + 1 + 2
                for k in range(K):
                    after_own(e.tensor_tensor_scan(change[:, k, 1:], decay_t[:, k, 0:L - 1], gap[:, k, 1:],
                                                   0.0, ALU.mult, ALU.add))
                signals += K
                e.tensor_tensor(c_start[:, :, 1:], c_start[:, :, 1:], change[:, :, 1:],
                                ALU.add).then_inc(s_cs, 1)
                e.memset(decay[0:L], 1.0).then_inc(s_fresh, 1)
                e.wait_ge(s_tcs, r + 1)
                after_own(e.tensor_tensor(h_start[:, :, 1:], out_gate_t[:, :, 0:L - 1], tc_start[:, :, 1:],
                                          ALU.mult))
                after_own(e.tensor_copy(hT[:, :, :], h_start[:, :, :]))
                after_own(e.tensor_copy(hTr[:, :, :], h_start[:, :, :]))
                signals += 3
                e.wait_ge(s_back, r + 1)
                e.tensor_copy(c[0:L].rearrange("c a u -> c (a u)"), back[0:L, :]).then_inc(s_begin, 1)
                e.wait_ge(s_begin, r + 2)
                e.sem_inc(s_own, (FINE_OWN if fine else ROUGH_OWN) - signals)
            all_rounds(e, one_round, s_apart)


_INS = ["x", "src", "dst", "L0_gnn_W1", "L0_gnn_b1", "L0_gnn_W2", "L0_gnn_b2",
        "L0_ffn_W_f", "L0_ffn_W_i", "L0_ffn_W_c", "L0_ffn_W_o",
        "L0_ffn_b_f", "L0_ffn_b_i", "L0_ffn_b_c", "L0_ffn_b_o"]


def kernel(**inputs):
    import numpy as _np
    import concourse.bacc as _bacc
    from concourse import mybir as _mybir
    from concourse.bass_utils import run_bass_kernel_spmd as _run

    nc = _bacc.Bacc("TRN2", target_bir_lowering=False, num_devices=1)
    arrays, args = {}, []
    for name in _INS:
        a = _np.ascontiguousarray(inputs[name])
        arrays[f"in_{name}_dram"] = a
        args.append(nc.dram_tensor(f"in_{name}_dram", a.shape, _mybir.dt.from_np(a.dtype),
                                   kind="ExternalInput").ap())
    shape = tuple(inputs["x"].shape)
    out = nc.dram_tensor("out_0_dram", shape, _mybir.dt.float32, kind="ExternalOutput").ap()
    x, src, dst, W1, b1, W2, b2 = args[:7]
    program(nc, x, src, dst, W1, b1, W2, b2, args[7:11], args[11:15], out)
    r = _run(nc, [arrays], core_ids=[0])
    return r.results[0]["out_0_dram"]
```

```python
from contextlib import ExitStack

import concourse.bass as bass
from concourse import mybir

F32 = mybir.dt.float32
F32R = mybir.dt.float32r
BF16 = mybir.dt.bfloat16
I32 = mybir.dt.int32
ALU = mybir.AluOpType
ACT = mybir.ActivationFunctionType
AX_X = mybir.AxisListType.X

P = 128
EPS = 1e-5
LANES = 125
GROUP = 9
LEAST_GROUPS = 2
PARTS = 3
LOAD_BLOCKS = 5
ROUGH = 2
FINE = 2
TOLERANCE = 2.0 ** -17


def program(nc, x, src, dst, W1, b1, W2, b2, Wg, bg, y):
    N, D = x.shape
    E, = src.shape
    K = D // P
    BLOCKS = N // LANES
    TILES = E // LANES
    STEPS = N // LANES
    G4 = 4 * D
    HALF = D // 2
    KH = K // 2
    PAIR = 2 * HALF
    assert N == BLOCKS * LANES and E == TILES * LANES and STEPS % 2 == 0 and PAIR == 512
    TPP = 8
    TROWS = TILES // TPP
    assert TROWS * TPP == TILES and TROWS <= P and BLOCKS <= P
    MORE = 2 * LANES

    table = nc.dram_tensor("ln_table", (N, D), F32, kind="Internal").ap()
    x1_rows = nc.dram_tensor("x1_rows", (N, D), F32, kind="Internal").ap()
    gate_rows = nc.dram_tensor("gate_rows", (N, G4), F32, kind="Internal").ap()

    with ExitStack() as top:
        def sb(stack, name, shape, dt=F32):
            return stack.enter_context(nc.sbuf_tensor(name, shape, dt))

        def pb(stack, name, shape, dt=F32):
            return stack.enter_context(nc.psum_tensor(name, shape, dt))

        def sem(stack, name):
            return stack.enter_context(nc.semaphore(name))

        ident = sb(top, "ident", [P, P])
        Wh = sb(top, "Wh", [P, K, 2, 2, 2, HALF])
        s_wh = sem(top, "s_wh")

        def gate_columns(w_sb, first_row):
            for half in range(2):
                for n, (bank, slot) in enumerate(((0, 0), (0, 1), (1, 0), (1, 1))):
                    yield (w_sb[:, :, half, bank, slot, :],
                           Wg[n][first_row:first_row + D, half * HALF:(half + 1) * HALF]
                           .rearrange("(k p) c -> p k c", p=P))

        WH_LOADS = 8

        with ExitStack() as first:
            src_cols = sb(first, "src_cols", [P, TILES + LEAST_GROUPS * GROUP], I32)
            dst_cols = sb(first, "dst_cols", [P, TILES + LEAST_GROUPS * GROUP])
            lo_row = sb(first, "lo_row", [1, BLOCKS], I32)
            extra_row = sb(first, "extra_row", [1, BLOCKS], I32)
            before_row = sb(first, "before_row", [1, BLOCKS], I32)

            table_part(nc, x, src, dst, table, ident, src_cols, dst_cols, lo_row, extra_row, before_row,
                       sb, pb, sem, N, D, TILES, BLOCKS, TPP, TROWS)
            graph_part(nc, x, table, x1_rows, gate_rows, W1, b1, W2, b2, bg, Wh, s_wh, gate_columns,
                       ident, src_cols, dst_cols, lo_row, extra_row, before_row,
                       sb, pb, sem, D, K, BLOCKS, TILES, G4, HALF, PAIR)
        lstm_part(nc, x1_rows, gate_rows, y, Wh, s_wh, WH_LOADS, ident,
                  sb, pb, sem, D, K, KH, STEPS, G4, HALF, PAIR, MORE)


def hold(e, passed, sem, value):
    e.wait_ge(sem, value)
    e.sem_inc(passed, 1)


def rsqrt_on_vector(e, after_own, var, root, r, t, s_root, roots, s_ready):
    e.wait_ge(s_root, roots)
    after_own(e.reciprocal(r, root))
    after_own(e.tensor_tensor(t, r, r, ALU.mult))
    after_own(e.tensor_tensor(t, t, var, ALU.mult))
    after_own(e.tensor_scalar(t, t, -0.5, 1.5, ALU.mult, ALU.add))
    after_own(e.tensor_tensor(r, r, t, ALU.mult))


def table_part(nc, x, src, dst, table, ident, src_cols, dst_cols, lo_row, extra_row, before_row,
               sb, pb, sem, N, D, TILES, BLOCKS, TPP, TROWS):
    LB = LOAD_BLOCKS
    GROUPS = BLOCKS // LB
    assert GROUPS * LB == BLOCKS and GROUPS % 2 == 0
    x_v = x.rearrange("(g j p) d -> g p j d", j=LB, p=LANES)
    table_v = table.rearrange("(g j p) d -> g p j d", j=LB, p=LANES)
    ETILE = LANES
    QUAD = 4

    with ExitStack() as ctx:
        xin = sb(ctx, "xin", [P, 2, LB, D])
        xout = sb(ctx, "xout", [P, 2, LB, D])
        stats = sb(ctx, "stats", [P, LB, 6])
        mv = sb(ctx, "mv", [P, LB, 2])
        ve = sb(ctx, "ve", [P, LB])
        root = sb(ctx, "root", [P, LB])
        rs = sb(ctx, "rs", [P, LB])
        rt = sb(ctx, "rt", [P, LB])
        raw_i = sb(ctx, "raw_i", [TROWS, 2, TPP * ETILE], I32)
        raw_f = sb(ctx, "raw_f", [TROWS, 2, TPP * ETILE])
        tmin = sb(ctx, "tmin", [TROWS, TPP])
        tmax = sb(ctx, "tmax", [TROWS, TPP])
        tile_no = sb(ctx, "tile_no", [TROWS, TPP])
        tile_up = sb(ctx, "tile_up", [TROWS, TPP])
        block_at = sb(ctx, "block_at", [TROWS, BLOCKS])
        key = sb(ctx, "key", [TROWS, TPP, BLOCKS])
        keys = sb(ctx, "keys", [TROWS, 2, TPP, BLOCKS])
        far = sb(ctx, "far", [TROWS, 2, BLOCKS])
        ends = sb(ctx, "ends", [BLOCKS, 2])
        row = sb(ctx, "row", [1, 8, BLOCKS])
        ones_row = sb(ctx, "ones_row", [1, BLOCKS])
        turned = [pb(ctx, f"turned{n}", [P, QUAD, TROWS]) for n in range(4)]
        far_t = pb(ctx, "far_t", [BLOCKS, 2, TROWS])
        ends_t = pb(ctx, "ends_t", [1, 2, BLOCKS])

        s_x = [sem(ctx, f"s_x{n}") for n in range(2)]
        s_out = [sem(ctx, f"s_out{n}") for n in range(2)]
        s_raw = sem(ctx, "s_raw")
        s_ident = sem(ctx, "s_ident")
        s_ids = sem(ctx, "s_ids")
        s_own = sem(ctx, "s_own")
        s_var = sem(ctx, "s_var")
        s_root = sem(ctx, "s_root")
        s_norm = sem(ctx, "s_norm")
        s_float = sem(ctx, "s_float")
        s_turn = sem(ctx, "s_turn")
        s_far = sem(ctx, "s_far")
        s_far_t = sem(ctx, "s_far_t")
        s_ends = sem(ctx, "s_ends")
        s_ends_t = sem(ctx, "s_ends_t")

        block = ctx.enter_context(nc.Block())

        @block.sync
        def _(e):
            e.dma_start(raw_i[:, 0, :], src.rearrange("(p n) -> p n", p=TROWS)).then_inc(s_raw, 16)
            e.dma_start(raw_i[:, 1, :], dst.rearrange("(p n) -> p n", p=TROWS)).then_inc(s_raw, 16)
            for g in range(GROUPS):
                if g >= 2:
                    e.wait_ge(s_norm, g - 1)
                e.dma_start(xin[0:LANES, g % 2], x_v[g]).then_inc(s_x[g % 2], 16)
                if g >= 1:
                    e.wait_ge(s_norm, g)
                    e.dma_start(table_v[g - 1], xout[0:LANES, (g - 1) % 2]).then_inc(s_out[(g - 1) % 2], 16)
            e.wait_ge(s_norm, GROUPS)
            e.dma_start(table_v[GROUPS - 1], xout[0:LANES, (GROUPS - 1) % 2]).then_inc(s_out[(GROUPS - 1) % 2], 16)
            for n in range(2):
                e.wait_ge(s_out[n], 16 * (GROUPS // 2))

        @block.gpsimd
        def _(e):
            e.memset(ident[:, :], 0.0).then_inc(s_ident, 1)
            e.wait_ge(s_ident, 1)
            e.affine_select(out=ident[:, :], in_=ident[:, :], compare_op=ALU.not_equal, fill=1.0,
                            base=0, pattern=[[-1, P]], channel_multiplier=1).then_inc(s_ident, 1)
            e.memset(src_cols[:, TILES:], 0).then_inc(s_ids, 1)
            e.memset(dst_cols[:, TILES:], -1.0).then_inc(s_ids, 1)
            e.iota(block_at[:, :], pattern=[[LANES, BLOCKS]], base=0, channel_multiplier=0,
                   allow_small_or_imprecise_dtypes=True).then_inc(s_ids, 1)
            e.iota(tile_no[:, :], pattern=[[1, TPP]], base=1, channel_multiplier=TPP,
                   allow_small_or_imprecise_dtypes=True).then_inc(s_ids, 1)

        @block.scalar
        def _(e):
            for g in range(GROUPS):
                e.wait_ge(s_var, g + 1)
                e.activation(root[0:LANES, :], ve[0:LANES, :], ACT.Sqrt).then_inc(s_root, 1)

        @block.tensor
        def _(e):
            e.wait_ge(s_ident, 2)
            e.wait_ge(s_float, 1)
            for which in range(2):
                for j in range(TPP):
                    t = e.transpose(turned[2 * which + j // QUAD][0:ETILE, j % QUAD, :],
                                    raw_f[:, which, j * ETILE:(j + 1) * ETILE], ident[0:TROWS, 0:TROWS])
            t.then_inc(s_turn, 1)
            e.wait_ge(s_far, 1)
            for n in range(2):
                t = e.transpose(far_t[:, n, :], far[:, n, :], ident[0:TROWS, 0:TROWS])
            t.then_inc(s_far_t, 1)
            e.wait_ge(s_ends, 1)
            for n in range(2):
                t = e.transpose(ends_t[:, n, :], ends[:, n:n + 1], ident[0:BLOCKS, 0:BLOCKS])
            t.then_inc(s_ends_t, 1)

        @block.vector
        def _(e):
            own = [0]

            def after_own(ins):
                own[0] += 1
                ins.then_inc(s_own, 1)
                e.wait_ge(s_own, own[0])

            e.wait_ge(s_raw, 32)
            e.tensor_copy(raw_f[:, :, :], raw_i[:, :, :]).then_inc(s_float, 1)
            e.wait_ge(s_float, 1)
            dst_tiles = raw_f[:, 1, :].rearrange("p (j n) -> p j n", j=TPP)
            after_own(e.tensor_reduce(tmin[:, :], dst_tiles, AX_X, ALU.min))
            after_own(e.tensor_reduce(tmax[:, :], dst_tiles, AX_X, ALU.max))
            e.wait_ge(s_turn, 1)
            for which, cols in ((0, src_cols), (1, dst_cols)):
                by_tile = cols[0:ETILE, 0:TILES].rearrange("e (p j) -> e j p", j=TPP)
                for q in range(TPP // QUAD):
                    after_own(e.tensor_copy(by_tile[:, q * QUAD:(q + 1) * QUAD, :],
                                            turned[2 * which + q][0:ETILE, :, :]))

            e.wait_ge(s_ids, 4)
            after_own(e.tensor_scalar(tile_up[:, :], tile_no[:, :], -1.0, float(TILES + 1), ALU.mult, ALU.add))
            after_own(e.tensor_scalar(tmin[:, :], tmin[:, :], float(LANES), None, ALU.subtract))
            for n, number in enumerate((tile_no, tile_up)):
                for j in range(TPP):
                    after_own(e.tensor_scalar(key[:, j, :], block_at[:, :], tmin[:, j:j + 1],
                                              number[:, j:j + 1], ALU.is_gt, ALU.mult))
                    after_own(e.scalar_tensor_tensor(out=keys[:, n, j, :], in0=block_at[:, :],
                                                     scalar=tmax[:, j:j + 1], in1=key[:, j, :],
                                                     op0=ALU.is_le, op1=ALU.mult))
                r = e.tensor_reduce(far[:, n, :], keys[:, n].rearrange("p j b -> p b j"), AX_X, ALU.max)
                if n == 0:
                    after_own(r)
            r.then_inc(s_far, 1)
            e.wait_ge(s_far_t, 1)
            e.tensor_reduce(ends[:, :], far_t[:, :, :], AX_X, ALU.max).then_inc(s_ends, 1)
            e.wait_ge(s_ends_t, 1)
            after_own(e.tensor_copy(row[:, 0:2, :], ends_t[:, :, :]))
            end, low, count = row[:, 0, :], row[:, 2, :], row[:, 3, :]
            after_own(e.tensor_scalar(low, row[:, 1, :], -1.0, float(TILES), ALU.mult, ALU.add))
            after_own(e.tensor_tensor(count, end, low, ALU.subtract))
            groups, upto = row[:, 4, :], row[:, 5, :]
            after_own(e.tensor_scalar(count, count, (GROUP - 1) / 2, 1.0 / GROUP, ALU.add, ALU.mult))
            after_own(e.tensor_scalar_add(count, count, 1.5 * 2.0 ** 23))
            after_own(e.tensor_scalar(groups, count, 1.5 * 2.0 ** 23, float(LEAST_GROUPS), ALU.subtract, ALU.max))
            after_own(e.tensor_scalar(extra_row[:, :], groups, float(LEAST_GROUPS), None, ALU.subtract))
            after_own(e.memset(ones_row[:, :], 1.0))
            after_own(e.tensor_tensor_scan(upto, groups, ones_row[:, :], 0.0, ALU.add, ALU.mult))
            after_own(e.tensor_tensor(row[:, 6, :], upto, groups, ALU.subtract))
            after_own(e.tensor_copy(before_row[:, :], row[:, 6, :]))
            after_own(e.tensor_copy(lo_row[:, :], low))

            for g in range(GROUPS):
                b = g % 2
                e.wait_ge(s_x[b], 16 * (g // 2 + 1))
                for j in range(LB):
                    e.bn_stats(stats[0:LANES, j, :], xin[0:LANES, b, j, :]).then_inc(s_own, 1)
                own[0] += LB
                e.wait_ge(s_own, own[0])
                for j in range(LB):
                    e.bn_aggr(mv[0:LANES, j, :], stats[0:LANES, j, :]).then_inc(s_own, 1)
                own[0] += LB
                e.wait_ge(s_own, own[0])
                e.tensor_scalar_add(ve[0:LANES, :], mv[0:LANES, :, 1], EPS).then_inc(s_var, 1)
                e.wait_ge(s_var, g + 1)
                rsqrt_on_vector(e, after_own, ve[0:LANES, :], root[0:LANES, :], rs[0:LANES, :],
                                rt[0:LANES, :], s_root, g + 1, None)
                if g >= 2:
                    e.wait_ge(s_out[b], 16 * (g // 2))
                for j in range(LB):
                    n = e.tensor_scalar(xout[0:LANES, b, j, :], xin[0:LANES, b, j, :], mv[0:LANES, j, 0:1],
                                        rs[0:LANES, j:j + 1], ALU.subtract, ALU.mult)
                    if j < LB - 1:
                        after_own(n)
                n.then_inc(s_norm, 1)
                e.wait_ge(s_norm, g + 1)


def graph_part(nc, x, table, x1_rows, gate_rows, W1, b1, W2, b2, bg, Wh, s_wh, gate_columns,
               ident, src_cols, dst_cols, lo_row, extra_row, before_row,
               sb, pb, sem, D, K, BLOCKS, TILES, G4, HALF, PAIR):
    x_v = x.rearrange("(b p) d -> b p d", p=LANES)
    table_v = table.rearrange("(b p) d -> b p d", p=LANES)
    x1_v = x1_rows.rearrange("(b p) d -> b p d", p=LANES)
    gate_v = gate_rows.rearrange("(b p) d -> b p d", p=LANES)
    L = LANES
    BANKS = G4 // PAIR

    with ExitStack() as ctx:
        Wx = sb(ctx, "Wx", [P, K, 2, 2, 2, HALF])
        W1s = sb(ctx, "W1s", [P, K, D])
        W2s = sb(ctx, "W2s", [P, K, D])
        b1c = sb(ctx, "b1c", [P, K])
        b2r = sb(ctx, "b2r", [P, D])
        bgr = sb(ctx, "bgr", [P, BANKS, PAIR])
        zeros = sb(ctx, "zeros", [1, D], BF16)
        node_id = sb(ctx, "node_id", [P, L])
        idx = [sb(ctx, f"idx{n}", [P, GROUP], I32) for n in range(LEAST_GROUPS + 1)]
        rows = [sb(ctx, f"rows{j}", [P, D]) for j in range(GROUP)]
        high = [sb(ctx, f"high{j}", [P, D], F32R) for j in range(PARTS)]
        low_part = [sb(ctx, f"low_part{j}", [P, D], F32R) for j in range(PARTS)]
        onehot = [sb(ctx, f"onehot{j}", [P, L], F32R) for j in range(PARTS)]
        xt = sb(ctx, "xt", [P, D])
        nt = sb(ctx, "nt", [P, D])
        hin = sb(ctx, "hin", [P, D])
        hinT = sb(ctx, "hinT", [P, K, L])
        h1T = sb(ctx, "h1T", [P, K, L])
        h2 = sb(ctx, "h2", [P, D])
        x1 = sb(ctx, "x1", [P, D])
        z = sb(ctx, "z", [P, D])
        zT = sb(ctx, "zT", [P, K, L])
        gout = sb(ctx, "gout", [P, 2, 2, PAIR])
        stats = sb(ctx, "gstats", [P, 6])
        mv = sb(ctx, "gmv", [P, 2])
        ve = sb(ctx, "gve", [P, 1])
        root = sb(ctx, "groot", [P, 1])
        rs = sb(ctx, "grs", [P, 1])
        rt = sb(ctx, "grt", [P, 1])
        agg = pb(ctx, "agg", [P, D])
        turned = pb(ctx, "rows_turned", [P, K, L])
        mid = [pb(ctx, f"mid{n}", [P, K // 2, L]) for n in range(2)]
        late = pb(ctx, "late", [P, D])
        gps = [pb(ctx, f"gps{n}", [P, PAIR]) for n in range(2)]

        s_w = sem(ctx, "s_w")
        s_xt = sem(ctx, "s_xt")
        s_nt = sem(ctx, "s_nt")
        s_zero = sem(ctx, "s_zero")
        s_rows = [sem(ctx, f"s_rows{j}") for j in range(GROUP)]
        s_idx = sem(ctx, "s_idx")
        s_hot = sem(ctx, "s_hot")
        s_high = sem(ctx, "s_high")
        s_low = sem(ctx, "s_low")
        s_visit = sem(ctx, "s_visit")
        s_agg = sem(ctx, "s_agg")
        s_hin = sem(ctx, "s_hin")
        s_hin_t = sem(ctx, "s_hin_t")
        s_hinT = sem(ctx, "s_hinT")
        s_mid = [sem(ctx, f"s_mid{m}") for m in range(2)]
        s_h1 = [sem(ctx, f"s_h1{m}") for m in range(K)]
        s_late = sem(ctx, "s_late")
        s_own = sem(ctx, "s_gown")
        s_passed = sem(ctx, "s_gpassed")
        s_x1 = sem(ctx, "s_x1")
        s_var = sem(ctx, "s_gvar")
        s_root = sem(ctx, "s_groot")
        s_z = sem(ctx, "s_z")
        s_z_t = sem(ctx, "s_z_t")
        s_zT = sem(ctx, "s_zT")
        s_gps = [sem(ctx, f"s_gps{n}") for n in range(BANKS)]
        s_gout = [sem(ctx, f"s_gout{n}") for n in range(BANKS)]
        s_x1_st = sem(ctx, "s_x1_st")
        s_g_st = [sem(ctx, f"s_g_st{n}") for n in range(2)]

        WEIGHT_LOADS = 8 + 2 + 1 + 1 + 8
        block = ctx.enter_context(nc.Block())

        def wait(e, semaphore, value):
            if not isinstance(value, int) or value > 0:
                e.wait_ge(semaphore, value)

        def all_iterations(e, one):
            one(0, True, False, False)
            one(1, True, True, False)
            one(2, True, True, True)
            with e.Fori(3, BLOCKS) as i:
                one(i, True, True, True)
            one(BLOCKS, False, True, True)
            one(BLOCKS + 1, False, False, True)

        def no_visits(*_):
            pass

        def block_visits(e, b, visit, with_column=False):
            extra = e.value_load(extra_row[0:1, bass.ds(b, 1)], min_val=0, max_val=-(-TILES // GROUP))
            before = e.value_load(before_row[0:1, bass.ds(b, 1)], min_val=0, max_val=BLOCKS * TILES)
            low = None
            if with_column:
                low = e.value_load(lo_row[0:1, bass.ds(b, 1)], min_val=0, max_val=TILES)

            def group(g, first, last, slab):
                for j in range(first, last):
                    column = None
                    if with_column:
                        column = nc.s_assert_within(
                            low + g * GROUP + j, 0, TILES + (LEAST_GROUPS - 1) * GROUP + j,
                            skip_runtime_bounds_check_because="a range ends at TILES, rounded up to the groups")
                    visit(before + g, j, column, slab)

            def beyond():
                with e.If(extra > 0):
                    with e.Fori(0, extra) as g:
                        group(g, 0, GROUP, LEAST_GROUPS)

            def some(first, last):
                for n in range(LEAST_GROUPS):
                    begin, end = max(first, n * GROUP), min(last, (n + 1) * GROUP)
                    if begin < end:
                        group(extra + n, begin - n * GROUP, end - n * GROUP, n)
            return beyond, some

        @block.sync
        def _(e):
            with nc.allow_non_contiguous_dma(reason="small bias column"):
                e.dma_start(b1c[:, :], b1.rearrange("(m p) -> p m", p=P)).then_inc(s_w, 16)
            e.dma_start(b2r[:, :], b2.rearrange("(o d) -> o d", o=1).to_broadcast([P, D])).then_inc(s_w, 16)
            e.dma_start(W1s[:, :, :], W1.rearrange("(k p) c -> p k c", p=P)).then_inc(s_w, 16)
            e.dma_start(W2s[:, :, :], W2.rearrange("(k p) c -> p k c", p=P)).then_inc(s_w, 16)
            for dst_ap, src_ap in gate_columns(Wx, 0):
                e.dma_start(dst_ap, src_ap).then_inc(s_w, 16)
            for half in range(2):
                for n, (bank, slot) in enumerate(((0, 0), (0, 1), (1, 0), (1, 1))):
                    e.dma_start(bgr[:, 2 * half + bank, slot * HALF:(slot + 1) * HALF],
                                bg[n][half * HALF:(half + 1) * HALF].rearrange("(o d) -> o d", o=1)
                                .to_broadcast([P, HALF])).then_inc(s_w, 16)

            def store_gates(b, half):
                for n in range(2):
                    e.wait_ge(s_gout[2 * half + n], b + 1)
                e.dma_start(gate_v[b][:, half * 2 * PAIR:(half + 1) * 2 * PAIR],
                            gout[0:L, half]).then_inc(s_g_st[half], 16)

            def one(i, tiles, layers, gates):
                if tiles:
                    wait(e, s_hin, i)
                    e.dma_start(nt[0:L, :], table_v[i]).then_inc(s_nt, 16)
                if layers:
                    wait(e, s_x1, i - 1)
                    e.dma_start(xt[0:L, :], x_v[i - 1]).then_inc(s_xt, 16)
                if gates:
                    store_gates(i - 2, 0)
                if layers:
                    e.wait_ge(s_x1, i)
                    e.dma_start(x1_v[i - 1], x1[0:L, :]).then_inc(s_x1_st, 16)
                if gates:
                    store_gates(i - 2, 1)
                if isinstance(i, int) and i == 0:
                    for dst_ap, src_ap in gate_columns(Wh, D):
                        e.dma_start(dst_ap, src_ap).then_inc(s_wh, 16)

            all_iterations(e, one)
            e.wait_ge(s_x1_st, 16 * BLOCKS)
            for half in range(2):
                e.wait_ge(s_g_st[half], 16 * BLOCKS)

        @block.gpsimd
        def _(e):
            def gather(q, j, column, slab):
                n = q * GROUP + j
                if j == 0:
                    if slab == LEAST_GROUPS:
                        e.wait_ge(s_low, n + GROUP)
                    else:
                        e.wait_ge(s_low, n + 1)
                    e.tensor_copy(idx[slab][0:L, :], src_cols[0:L, bass.ds(column, GROUP)]).then_inc(s_idx, 1)
                    hold(e, s_passed, s_idx, q + 1)
                else:
                    hold(e, s_passed, s_low, n + 1)
                e.indirect_dma_start(
                    out=rows[j][0:L, :], out_offset=None, in_=table[:, :],
                    in_offset=bass.IndirectOffsetOnAxis(ap=idx[slab][0:L, j:j + 1], axis=0),
                ).then_inc(s_rows[j], 16)

            with e.Fori(0, BLOCKS) as b:
                beyond, some = block_visits(e, b, gather, True)
                beyond()
                some(0, LEAST_GROUPS * GROUP)

        @block.scalar
        def _(e):
            def high_part(q, j, column, slab):
                n = q * GROUP + j
                e.wait_ge(s_rows[j], (q + 1) * 16)
                e.wait_ge(s_visit, n + 1)
                e.activation(high[j % PARTS][0:L, :], rows[j][0:L, :], ACT.Copy).then_inc(s_high, 1)

            def one(i, tiles, layers, gates):
                beyond, some = block_visits(e, i, high_part) if tiles else (no_visits, no_visits)
                beyond()
                some(0, 3)
                if layers:
                    e.wait_ge(s_hin_t, i)
                    e.activation(hinT[:, :, :], turned[:, :, :], ACT.Copy).then_inc(s_hinT, 1)
                some(3, 6)
                if layers:
                    for m in range(K):
                        e.wait_ge(s_mid[m // 2], i)
                        e.activation(h1T[:, m, :], mid[m // 2][:, m % 2, :], ACT.Relu,
                                     bias=b1c[:, m:m + 1]).then_inc(s_h1[m], 1)
                some(6, 9)
                if layers:
                    e.wait_ge(s_var, i)
                    e.activation(root[0:L, :], ve[0:L, :], ACT.Sqrt).then_inc(s_root, 1)
                some(9, 15)
                if layers:
                    e.wait_ge(s_z_t, i)
                    e.activation(zT[:, :, :], turned[:, :, :], ACT.Copy).then_inc(s_zT, 1)
                some(15, 18)

            e.wait_ge(s_w, 16 * WEIGHT_LOADS)
            all_iterations(e, one)

        @block.tensor
        def _(e):
            def visit(q, j, column, slab):
                n = q * GROUP + j
                e.wait_ge(s_hot, n + 1)
                e.wait_ge(s_low, n + 1 + GROUP)
                for part in (high, low_part):
                    m = e.matmul(agg[0:L, :], onehot[j % PARTS][0:L, :], part[j % PARTS][0:L, :],
                                 start=False, stop=False, skip_group_check=True)
                m.then_inc(s_visit, 1)

            def turn(rows_of):
                for k in range(K):
                    t = e.transpose(turned[:, k, :], rows_of[0:L, k * P:(k + 1) * P], ident[0:L, 0:L])
                return t

            def gate_bank(b, n):
                if n >= 2:
                    e.wait_ge(s_gout[n - 2], b + 1)
                else:
                    wait(e, s_gout[n + 2], b)
                for k in range(K):
                    m = e.matmul(gps[n % 2][0:L, :], zT[:, k, :],
                                 Wx[:, k, n // 2, n % 2].rearrange("p s c -> p (s c)"),
                                 start=(k == 0), stop=(k == K - 1))
                m.then_inc(s_gps[n], 1)

            def one(i, tiles, layers, gates):
                beyond, some = block_visits(e, i, visit) if tiles else (no_visits, no_visits)
                wait(e, s_hin, i if tiles or layers else 0)
                if layers:
                    wait(e, s_zT, i - 1)
                    turn(hin).then_inc(s_hin_t, 1)
                if tiles:
                    e.matmul(agg[0:L, :], zeros[0:1, 0:L], zeros[0:1, :], start=True, stop=False,
                             skip_group_check=True)
                beyond()
                some(0, 3)
                if layers:
                    e.wait_ge(s_hinT, i)
                    for m in range(K):
                        for k in range(K):
                            mm = e.matmul(mid[m // 2][:, m % 2, :], W1s[:, k, m * P:(m + 1) * P], hinT[:, k, :],
                                          start=(k == 0), stop=(k == K - 1))
                        if m % 2:
                            mm.then_inc(s_mid[m // 2], 1)
                some(3, 6)
                if layers:
                    for k in range(K):
                        e.wait_ge(s_h1[k], i)
                        mm = e.matmul(late[0:L, :], h1T[:, k, :], W2s[:, k, :], start=(k == 0), stop=(k == K - 1))
                    mm.then_inc(s_late, 1)
                if gates:
                    gate_bank(i - 2, 2)
                some(6, 9)
                if gates:
                    gate_bank(i - 2, 3)
                some(9, 12)
                if layers:
                    e.wait_ge(s_z, i)
                    turn(z).then_inc(s_z_t, 1)
                some(12, 15)
                if layers:
                    e.wait_ge(s_zT, i)
                    gate_bank(i - 1, 0)
                some(15, 18)
                if tiles:
                    e.matmul(agg[0:L, :], zeros[0:1, 0:L], zeros[0:1, :], start=False, stop=True,
                             skip_group_check=True).then_inc(s_agg, 1)
                if layers:
                    gate_bank(i - 1, 1)

            e.wait_ge(s_w, 16 * WEIGHT_LOADS)
            e.wait_ge(s_zero, 1)
            e.sem_inc(s_visit, PARTS)
            all_iterations(e, one)

        @block.vector
        def _(e):
            OWN = 12

            def low_and_one_hot(q, j, column, slab):
                n = q * GROUP + j
                e.wait_ge(s_visit, n + 1)
                e.tensor_scalar(onehot[j % PARTS][0:L, :], node_id[0:L, :], dst_cols[0:L, bass.ds(column, 1)],
                                None, ALU.is_equal).then_inc(s_hot, 1)
                e.wait_ge(s_high, n + 1)
                e.tensor_tensor(low_part[j % PARTS][0:L, :], rows[j][0:L, :],
                                high[j % PARTS][0:L, :].bitcast(F32), ALU.subtract).then_inc(s_low, 1)

            def gate_biases(b, n):
                if n % 2 == 0:
                    wait(e, s_g_st[n // 2], b * 16)
                e.wait_ge(s_gps[n], b + 1)
                e.tensor_tensor(gout[0:L, n // 2, n % 2, :], gps[n % 2][0:L, :], bgr[0:L, n, :],
                                ALU.add).then_inc(s_gout[n], 1)

            def one(i, tiles, layers, gates):
                beyond, some = block_visits(e, i, low_and_one_hot, True) if tiles else (no_visits, no_visits)
                own = [i * OWN]

                def after_own(ins):
                    own[0] = own[0] + 1
                    ins.then_inc(s_own, 1)
                    e.wait_ge(s_own, own[0])

                if layers:
                    e.wait_ge(s_agg, i)
                    e.wait_ge(s_nt, i * 16)
                    wait(e, s_hin_t, i - 1)
                    e.tensor_tensor(hin[0:L, :], agg[0:L, :], nt[0:L, :], ALU.add).then_inc(s_hin, 1)
                beyond()
                some(0, 3)
                if gates:
                    gate_biases(i - 2, 1)
                some(3, 9)
                if layers:
                    e.wait_ge(s_late, i)
                    after_own(e.tensor_tensor(h2[0:L, :], late[0:L, :], b2r[0:L, :], ALU.add))
                    e.wait_ge(s_xt, i * 16)
                    wait(e, s_x1_st, (i - 1) * 16)
                    e.scalar_tensor_tensor(out=x1[0:L, :], in0=h2[0:L, :], scalar=0.0, in1=xt[0:L, :],
                                           op0=ALU.max, op1=ALU.add).then_inc(s_x1, 1)
                    e.wait_ge(s_x1, i)
                    e.bn_stats(stats[0:L, :], x1[0:L, :]).then_inc(s_own, 1)
                    own[0] = own[0] + 1
                    hold(e, s_passed, s_own, own[0])
                    after_own(e.bn_aggr(mv[0:L, :], stats[0:L, :]))
                    e.tensor_scalar_add(ve[0:L, :], mv[0:L, 1:2], EPS).then_inc(s_var, 1)
                if gates:
                    gate_biases(i - 2, 2)
                if layers:
                    e.wait_ge(s_var, i)
                    rsqrt_on_vector(e, after_own, ve[0:L, :], root[0:L, :], rs[0:L, :], rt[0:L, :],
                                    s_root, i, None)
                    wait(e, s_z_t, i - 1)
                    e.tensor_scalar(z[0:L, :], x1[0:L, :], mv[0:L, 0:1], rs[0:L, 0:1], ALU.subtract,
                                    ALU.mult).then_inc(s_z, 1)
                    e.wait_ge(s_z, i)
                some(9, 12)
                if gates:
                    gate_biases(i - 2, 3)
                some(12, 18)
                if tiles:
                    after_own(e.tensor_scalar_add(node_id[0:L, :], node_id[0:L, :], float(L)))
                e.sem_inc(s_own, OWN - (8 if layers else 0) - (1 if tiles else 0))
                if layers:
                    gate_biases(i - 1, 0)

            e.memset(zeros[:, :], 0.0).then_inc(s_zero, 1)
            e.sem_inc(s_low, GROUP)
            e.wait_ge(s_w, 16 * WEIGHT_LOADS)
            e.memset(node_id[0:L, :], 0.0).then_inc(s_zero, 1)
            e.memset(hin[0:L, 0:L], 1.0).then_inc(s_zero, 1)
            e.wait_ge(s_zero, 3)
            e.tensor_tensor_scan(node_id[0:L, :], hin[0:L, 0:L], hin[0:L, 0:L], -1.0, ALU.add,
                                 ALU.mult).then_inc(s_zero, 1)
            e.wait_ge(s_zero, 4)
            all_iterations(e, one)


def lstm_part(nc, x1_rows, gate_rows, y, Wh, s_wh, WH_LOADS, ident,
              sb, pb, sem, D, K, KH, STEPS, G4, HALF, PAIR, MORE):
    L = LANES
    AHEAD = 2
    gates_v = gate_rows.rearrange("(c t) g -> t c g", t=STEPS)
    x1_v = x1_rows.rearrange("(c t) d -> t c d", t=STEPS)
    y_v = y.rearrange("(c t) d -> t c d", t=STEPS)

    with ExitStack() as ctx:
        Wr = sb(ctx, "Wr", [P, K, 2, 2, 2, HALF], F32R)
        hT = sb(ctx, "hT", [P, K, L])
        hTr = sb(ctx, "hTr", [P, K, L], F32R)
        xg = [sb(ctx, f"xg{n}", [P, 2, 2, PAIR]) for n in range(2)]
        total = sb(ctx, "total", [P, 2, 2, PAIR])
        gate = sb(ctx, "gate", [P, 2, 2, 2, HALF])
        c = sb(ctx, "c", [P, 2, HALF])
        fc = sb(ctx, "fc", [P, 2, HALF])
        ic = sb(ctx, "ic", [P, 2, HALF])
        tc = sb(ctx, "tc", [P, 2, HALF])
        h = [sb(ctx, f"h{n}", [P, 2, HALF]) for n in range(2)]
        decay = sb(ctx, "decay", [P, 2, HALF])
        x1 = [sb(ctx, f"lx1{n}", [P, D]) for n in range(2)]
        out = [sb(ctx, f"out{n}", [P, D]) for n in range(2)]
        c_start = sb(ctx, "c_start", [P, K, L])
        h_start = sb(ctx, "h_start", [P, K, L])
        gap = sb(ctx, "gap", [P, K, L])
        h_gap = sb(ctx, "h_gap", [P, K, L])
        change = sb(ctx, "change", [P, K, L])
        tc_start = sb(ctx, "tc_start", [P, K, L])
        most = sb(ctx, "most", [P, 4])
        worst = sb(ctx, "worst", [P, 1])
        worst1 = sb(ctx, "worst1", [1, 2])
        apart = sb(ctx, "apart", [1, 1], I32)

        acc = [pb(ctx, f"acc{n}", [P, PAIR]) for n in range(4)]
        hturn = [pb(ctx, f"hturn{n}", [P, KH, L]) for n in range(2)]
        back = pb(ctx, "back", [P, D])
        worst_t = pb(ctx, "worst_t", [1, P])
        c_end_t, decay_t, out_gate_t = (acc[n][:, 0:K * L].rearrange("p (k l) -> p k l", k=K) for n in range(3))

        s_acc = [sem(ctx, f"s_acc{n}") for n in range(4)]
        s_sum = [sem(ctx, f"s_sum{n}") for n in range(4)]
        s_fi = [sem(ctx, f"s_fi{n}") for n in range(2)]
        s_ct = [sem(ctx, f"s_ct{n}") for n in range(2)]
        s_o = [sem(ctx, f"s_o{n}") for n in range(2)]
        s_prod = [sem(ctx, f"s_prod{n}") for n in range(2)]
        s_c = [sem(ctx, f"s_c{n}") for n in range(2)]
        s_tc = [sem(ctx, f"s_tc{n}") for n in range(2)]
        s_h = [sem(ctx, f"s_h{n}") for n in range(2)]
        s_turn = [sem(ctx, f"s_lturn{n}") for n in range(2)]
        s_hT = [sem(ctx, f"s_hT{n}") for n in range(2)]
        s_decay = [sem(ctx, f"s_decay{n}") for n in range(2)]
        s_xg = [sem(ctx, f"s_xg{n}") for n in range(2)]
        s_x1 = [sem(ctx, f"s_lx1{n}") for n in range(2)]
        s_out = sem(ctx, "s_lout")
        s_y = [sem(ctx, f"s_y{n}") for n in range(2)]
        s_init = sem(ctx, "s_init")
        s_own = sem(ctx, "s_lown")
        s_ends = sem(ctx, "s_lends")
        s_cs = sem(ctx, "s_cs")
        s_tcs = sem(ctx, "s_tcs")
        s_back = sem(ctx, "s_back")
        s_begin = sem(ctx, "s_begin")
        s_fresh = sem(ctx, "s_fresh")
        s_worst = sem(ctx, "s_worst")
        s_worst_t = sem(ctx, "s_worst_t")
        s_apart = sem(ctx, "s_apart")
        s_passed = sem(ctx, "s_lpassed")

        block = ctx.enter_context(nc.Block())

        def steps_of_round(e, r, step):
            base = r * STEPS + AHEAD + 1
            step(0, 0, base, True, False)
            with e.Fori(0, STEPS // 2 - 1) as i:
                step(i * 2 + 1, 1, base + i * 2 + 1, False, False)
                step(i * 2 + 2, 0, base + i * 2 + 2, False, False)
            step(STEPS - 1, 1, base + (STEPS - 1), False, True)

        def all_rounds(e, one_round, signal_anyway=None):
            with e.Fori(0, ROUGH) as r:
                one_round(r, False, False, r)
            for f in range(FINE - 1):
                one_round(ROUGH + f, True, False, f)
            one_round(ROUGH + FINE - 1, True, True, FINE - 1)

            def not_met(checks):
                hold(e, s_passed, s_apart, checks)
                return e.value_load(apart[0:1, 0:1], min_val=0, max_val=1)

            with e.If(not_met(FINE) == 1):
                with e.Fori(0, MORE) as m:
                    with e.If(not_met(m + FINE) == 1):
                        one_round(m + (ROUGH + FINE), True, True, m + FINE)
                    with e.Else():
                        if signal_anyway is not None:
                            e.sem_inc(signal_anyway, 1)

        @block.sync
        def _(e):
            for n in range(2):
                e.sem_inc(s_y[n], 16)
            def one_round(r, fine, writes, checked):
                def step(s, par, now, first, last):
                    e.wait_ge(s_sum[3], now - 2)
                    e.dma_start(xg[par][0:L].rearrange("c a b g -> c (a b g)"), gates_v[s]).then_inc(s_xg[par], 16)
                    if writes:
                        e.wait_ge(s_out, now - 2)
                        e.dma_start(x1[par][0:L, :], x1_v[s]).then_inc(s_x1[par], 16)
                        e.wait_ge(s_out, now)
                        e.dma_start(y_v[s], out[par][0:L, :]).then_inc(s_y[par], 16)
                steps_of_round(e, r, step)
                if writes:
                    written = (r - (ROUGH + FINE - 1) + 1) * (STEPS // 2)
                    for n in range(2):
                        hold(e, s_passed, s_y[n], written * 16 + 16)
            all_rounds(e, one_round)

        @block.gpsimd
        def _(e):
            for s in s_decay:
                e.sem_inc(s, AHEAD)
            e.sem_inc(s_out, AHEAD + (ROUGH + FINE - 1) * STEPS)

            def one_round(r, fine, writes, checked):
                e.wait_ge(s_fresh, r + 1)
                def step(s, par, now, first, last):
                    for half in range(2):
                        e.wait_ge(s_fi[half], now)
                        e.wait_ge(s_decay[half], now - 1)
                        e.tensor_tensor(decay[0:L, half], decay[0:L, half], gate[0:L, half, 0, 0],
                                        ALU.mult).then_inc(s_decay[half], 1)
                    if writes:
                        n = now - (AHEAD + 1) - (ROUGH + FINE - 1) * STEPS
                        e.wait_ge(s_x1[par], (n - par) * 8 + 16)
                        e.wait_ge(s_y[par], (n - par) * 8 + 16)
                        for half in range(2):
                            e.wait_ge(s_h[half], now)
                        e.tensor_tensor(out[par][0:L, :], h[par][0:L].rearrange("c a u -> c (a u)"),
                                        x1[par][0:L, :], ALU.add).then_inc(s_out, 1)
                steps_of_round(e, r, step)
            all_rounds(e, one_round)

        @block.scalar
        def _(e):
            for s in (*s_fi, *s_ct, *s_o, *s_tc, *s_hT):
                e.sem_inc(s, AHEAD)
            e.wait_ge(s_wh, 16 * WH_LOADS)
            e.activation(Wr[:, 0:1, 0, 0, 0, 0:2], Wh[:, 0:1, 0, 0, 0, 0:2], ACT.Sigmoid).then_inc(s_init, 1)
            e.wait_ge(s_init, 1)
            for k in range(K):
                e.activation(Wr[:, k], Wh[:, k], ACT.Copy).then_inc(s_init, 1)

            def one_round(r, fine, writes, checked):
                turned = hT if fine else hTr

                def take_turned(half, now):
                    e.wait_ge(s_turn[half], now)
                    e.activation(turned[:, half * KH:(half + 1) * KH, :], hturn[half][:, :, :],
                                 ACT.Copy).then_inc(s_hT[half], 1)

                def step(s, par, now, first, last):
                    if not first:
                        take_turned(1, now - 1)
                    else:
                        e.wait_ge(s_begin, r + 1)
                    def forget_input(half):
                        e.wait_ge(s_sum[2 * half], now)
                        e.wait_ge(s_decay[half], now - 1)
                        e.activation(gate[0:L, half, 0].rearrange("c s u -> c (s u)"), total[0:L, half, 0],
                                     ACT.Sigmoid).then_inc(s_fi[half], 1)

                    def cell_output(half):
                        e.wait_ge(s_sum[2 * half + 1], now)
                        e.activation(gate[0:L, half, 1, 0], total[0:L, half, 1, 0:HALF],
                                     ACT.Tanh).then_inc(s_ct[half], 1)
                        e.activation(gate[0:L, half, 1, 1], total[0:L, half, 1, HALF:PAIR],
                                     ACT.Sigmoid).then_inc(s_o[half], 1)

                    def new_cell(half):
                        e.wait_ge(s_c[half], now)
                        e.activation(tc[0:L, half], c[0:L, half], ACT.Tanh).then_inc(s_tc[half], 1)

                    forget_input(0)
                    cell_output(0)
                    new_cell(0)
                    forget_input(1)
                    take_turned(0, now)
                    cell_output(1)
                    new_cell(1)
                    if last:
                        take_turned(1, now)
                steps_of_round(e, r, step)
                e.wait_ge(s_cs, r + 1)
                e.activation(tc_start[:, :, :], c_start[:, :, :], ACT.Tanh).then_inc(s_tcs, 1)
            all_rounds(e, one_round)

        @block.tensor
        def _(e):
            for s in (*s_acc, *s_turn):
                e.sem_inc(s, AHEAD)
            e.wait_ge(s_init, 1 + K)

            def one_round(r, fine, writes, checked):
                state, weights = (hT, Wh) if fine else (hTr, Wr)

                def products(n, ks):
                    for k in ks:
                        m = e.matmul(acc[n][0:L, :], state[:, k, :],
                                     weights[:, k, n // 2, n % 2].rearrange("p s c -> p (s c)"),
                                     start=(k == 0), stop=(k == K - 1), skip_group_check=True)
                    return m

                def turn(half, par, now):
                    e.wait_ge(s_h[half], now)
                    for k in range(KH):
                        t = e.transpose(hturn[half][:, k, :], h[par][0:L, half, k * P:(k + 1) * P],
                                        ident[0:L, 0:L])
                    t.then_inc(s_turn[half], 1)

                def step(s, par, now, first, last):
                    if first:
                        e.wait_ge(s_begin, r + 1)
                    else:
                        e.wait_ge(s_hT[0], now - 1)
                    for n in range(4):
                        e.wait_ge(s_sum[n], now - 1)
                        products(n, range(KH))
                    if not first:
                        turn(1, 1 - par, now - 1)
                        e.wait_ge(s_hT[1], now - 1)
                    for n in range(3):
                        products(n, range(KH, K)).then_inc(s_acc[n], 1)
                    products(3, range(KH, K - 1))
                    turn(0, par, now)
                    products(3, range(K - 1, K)).then_inc(s_acc[3], 1)
                    if last:
                        turn(1, par, now)
                steps_of_round(e, r, step)

                now = (r + 1) * STEPS + AHEAD
                for half in range(2):
                    e.wait_ge(s_c[half], now)
                    e.wait_ge(s_decay[half], now)
                    e.wait_ge(s_o[half], now)
                for n in range(4):
                    e.wait_ge(s_sum[n], now)
                for to, of in ((c_end_t, c), (decay_t, decay), (out_gate_t, gate[:, :, 1, 1])):
                    for k in range(K):
                        u = (k % KH) * P
                        t = e.transpose(to[:, k, :], of[0:L, k // KH, u:u + P], ident[0:L, 0:L])
                t.then_inc(s_ends, 1)
                if fine:
                    e.wait_ge(s_worst, checked + 1)
                    e.transpose(worst_t[:, :], worst[:, :], ident[:, :]).then_inc(s_worst_t, 1)
                e.wait_ge(s_cs, r + 1)
                for k in range(K):
                    t = e.transpose(back[0:L, k * P:(k + 1) * P], c_start[:, k, :], ident[:, :])
                t.then_inc(s_back, 1)
            all_rounds(e, one_round)

        @block.vector
        def _(e):
            for s in (*s_sum, *s_c, *s_h):
                e.sem_inc(s, AHEAD)
            for s in s_prod:
                e.sem_inc(s, 2 * AHEAD)
            clear = (c, hT, c_start, h_start, gap, h_gap, change)
            for t in clear:
                e.memset(t[:, :, :], 0.0).then_inc(s_own, 1)
            e.memset(decay[:, :, :], 1.0).then_inc(s_fresh, 1)
            e.wait_ge(s_own, len(clear))
            e.tensor_copy(hTr[:, :, :], hT[:, :, :]).then_inc(s_begin, 1)
            CLEARED = len(clear)
            ROUGH_OWN, FINE_OWN = 12, 22

            def one_round(r, fine, writes, checked):
                def step(s, par, now, first, last):
                    count = now - (AHEAD + 1)
                    def add_inputs(n):
                        half, bank = n // 2, n % 2
                        e.wait_ge(s_acc[n], now)
                        if n == 0:
                            e.wait_ge(s_xg[par], (count - par) * 8 + 16)
                        if bank == 0:
                            e.wait_ge(s_fi[half], now - 1)
                        else:
                            e.wait_ge(s_o[half], now - 1)
                        e.tensor_tensor(total[0:L, half, bank], acc[n][0:L, :], xg[par][0:L, half, bank],
                                        ALU.add).then_inc(s_sum[n], 1)

                    def new_cell(half):
                        e.wait_ge(s_fi[half], now)
                        e.tensor_tensor(fc[0:L, half], gate[0:L, half, 0, 0], c[0:L, half],
                                        ALU.mult).then_inc(s_prod[half], 1)
                        e.wait_ge(s_ct[half], now)
                        e.tensor_tensor(ic[0:L, half], gate[0:L, half, 0, 1], gate[0:L, half, 1, 0],
                                        ALU.mult).then_inc(s_prod[half], 1)
                        e.wait_ge(s_prod[half], now * 2)
                        e.tensor_tensor(c[0:L, half], fc[0:L, half], ic[0:L, half],
                                        ALU.add).then_inc(s_c[half], 1)

                    def new_h(half):
                        e.wait_ge(s_o[half], now)
                        e.wait_ge(s_tc[half], now)
                        if writes and half == 0:
                            e.wait_ge(s_out, now - 1)
                        e.tensor_tensor(h[par][0:L, half], gate[0:L, half, 1, 1], tc[0:L, half],
                                        ALU.mult).then_inc(s_h[half], 1)

                    add_inputs(0)
                    add_inputs(1)
                    new_cell(0)
                    add_inputs(2)
                    new_h(0)
                    add_inputs(3)
                    new_cell(1)
                    new_h(1)
                steps_of_round(e, r, step)

                own = [(r - ROUGH) * FINE_OWN + ROUGH * ROUGH_OWN + CLEARED if fine
                       else r * ROUGH_OWN + CLEARED]

                def after_own(ins):
                    own[0] = own[0] + 1
                    ins.then_inc(s_own, 1)
                    e.wait_ge(s_own, own[0])

                signals = 0
                e.wait_ge(s_ends, r + 1)
                after_own(e.tensor_tensor(gap[:, :, 1:], c_end_t[:, :, 0:L - 1], c_start[:, :, 1:], ALU.subtract))
                signals += 1
                if fine:
                    for half in range(2):
                        e.wait_ge(s_hT[half], (r + 1) * STEPS + AHEAD)
                    after_own(e.tensor_tensor(h_gap[:, :, 1:], hT[:, :, 0:L - 1], h_start[:, :, 1:],
                                              ALU.subtract))
                    for n, (g, op) in enumerate(((gap, ALU.max), (h_gap, ALU.max), (gap, ALU.min), (h_gap, ALU.min))):
                        after_own(e.tensor_reduce(most[:, n:n + 1], g[:, :, :].rearrange("p k l -> p (k l)"),
                                                  AX_X, op))
                    after_own(e.tensor_scalar(most[:, 2:4], most[:, 2:4], -1.0, None, ALU.mult))
                    e.tensor_reduce(worst[:, :], most[:, :], AX_X, ALU.max).then_inc(s_worst, 1)
                    e.wait_ge(s_worst_t, checked + 1)
                    after_own(e.tensor_reduce(worst1[:, 0:1], worst_t[:, :], AX_X, ALU.max))
                    after_own(e.tensor_scalar(worst1[:, 1:2], worst1[:, 0:1], TOLERANCE, None, ALU.is_gt))
                    e.tensor_copy(apart[:, :], worst1[:, 1:2]).then_inc(s_apart, 1)
                    signals += 1 + 4 + 1 + 2
                for k in range(K):
                    after_own(e.tensor_tensor_scan(change[:, k, 1:], decay_t[:, k, 0:L - 1], gap[:, k, 1:],
                                                   0.0, ALU.mult, ALU.add))
                signals += K
                e.tensor_tensor(c_start[:, :, 1:], c_start[:, :, 1:], change[:, :, 1:],
                                ALU.add).then_inc(s_cs, 1)
                e.memset(decay[0:L], 1.0).then_inc(s_fresh, 1)
                e.wait_ge(s_tcs, r + 1)
                after_own(e.tensor_tensor(h_start[:, :, 1:], out_gate_t[:, :, 0:L - 1], tc_start[:, :, 1:],
                                          ALU.mult))
                after_own(e.tensor_copy(hT[:, :, :], h_start[:, :, :]))
                after_own(e.tensor_copy(hTr[:, :, :], h_start[:, :, :]))
                signals += 3
                e.wait_ge(s_back, r + 1)
                e.tensor_copy(c[0:L].rearrange("c a u -> c (a u)"), back[0:L, :]).then_inc(s_begin, 1)
                e.wait_ge(s_begin, r + 2)
                e.sem_inc(s_own, (FINE_OWN if fine else ROUGH_OWN) - signals)
            all_rounds(e, one_round, s_apart)


_INS = ["x", "src", "dst", "L0_gnn_W1", "L0_gnn_b1", "L0_gnn_W2", "L0_gnn_b2",
        "L0_ffn_W_f", "L0_ffn_W_i", "L0_ffn_W_c", "L0_ffn_W_o",
        "L0_ffn_b_f", "L0_ffn_b_i", "L0_ffn_b_c", "L0_ffn_b_o"]


def kernel(**inputs):
    import numpy as _np
    import concourse.bacc as _bacc
    from concourse import mybir as _mybir
    from concourse.bass_utils import run_bass_kernel_spmd as _run

    nc = _bacc.Bacc("TRN2", target_bir_lowering=False, num_devices=1)
    arrays, args = {}, []
    for name in _INS:
        a = _np.ascontiguousarray(inputs[name])
        arrays[f"in_{name}_dram"] = a
        args.append(nc.dram_tensor(f"in_{name}_dram", a.shape, _mybir.dt.from_np(a.dtype),
                                   kind="ExternalInput").ap())
    shape = tuple(inputs["x"].shape)
    out = nc.dram_tensor("out_0_dram", shape, _mybir.dt.float32, kind="ExternalOutput").ap()
    x, src, dst, W1, b1, W2, b2 = args[:7]
    program(nc, x, src, dst, W1, b1, W2, b2, args[7:11], args[11:15], out)
    r = _run(nc, [arrays], core_ids=[0])
    return r.results[0]["out_0_dram"]
```

```python
from contextlib import ExitStack

import concourse.bass as bass
from concourse import mybir

F32 = mybir.dt.float32
F32R = mybir.dt.float32r
I32 = mybir.dt.int32
ALU = mybir.AluOpType
ACT = mybir.ActivationFunctionType
AX_X = mybir.AxisListType.X

P = 128
EPS = 1e-5
LANES = 125
GROUP = 9
LEAST_GROUPS = 2
PARTS = 3
LOAD_BLOCKS = 5
ROUGH = 2
FINE = 2
TOLERANCE = 2.0 ** -17


def program(nc, x, src, dst, W1, b1, W2, b2, Wg, bg, y):
    N, D = x.shape
    E, = src.shape
    K = D // P
    BLOCKS = N // LANES
    TILES = E // LANES
    STEPS = N // LANES
    G4 = 4 * D
    HALF = D // 2
    KH = K // 2
    PAIR = 2 * HALF
    assert N == BLOCKS * LANES and E == TILES * LANES and STEPS % 2 == 0 and PAIR == 512
    TPP = 8
    TROWS = TILES // TPP
    assert TROWS * TPP == TILES and TROWS <= P and BLOCKS <= P
    MORE = 2 * LANES

    table = nc.dram_tensor("ln_table", (N, D), F32, kind="Internal").ap()
    x1_rows = nc.dram_tensor("x1_rows", (N, D), F32, kind="Internal").ap()
    gate_rows = nc.dram_tensor("gate_rows", (N, G4), F32, kind="Internal").ap()

    with ExitStack() as top:
        def sb(stack, name, shape, dt=F32):
            return stack.enter_context(nc.sbuf_tensor(name, shape, dt))

        def pb(stack, name, shape, dt=F32):
            return stack.enter_context(nc.psum_tensor(name, shape, dt))

        def sem(stack, name):
            return stack.enter_context(nc.semaphore(name))

        ident = sb(top, "ident", [P, P])
        Wh = sb(top, "Wh", [P, K, 2, 2, 2, HALF])
        s_wh = sem(top, "s_wh")

        def gate_columns(w_sb, first_row):
            for half in range(2):
                for n, (bank, slot) in enumerate(((0, 0), (0, 1), (1, 0), (1, 1))):
                    yield (w_sb[:, :, half, bank, slot, :],
                           Wg[n][first_row:first_row + D, half * HALF:(half + 1) * HALF]
                           .rearrange("(k p) c -> p k c", p=P))

        WH_LOADS = 8

        with ExitStack() as first:
            src_cols = sb(first, "src_cols", [P, TILES + LEAST_GROUPS * GROUP], I32)
            dst_cols = sb(first, "dst_cols", [P, TILES + LEAST_GROUPS * GROUP])
            ranges = sb(first, "ranges", [1, BLOCKS, 4], I32)
            Wx = Parts(*(sb(first, f"Wx_{part}", [P, K, 2, 2, 2, HALF], F32R) for part in ("high", "low")))
            W1s = sb(first, "W1s", [P, K, D])
            W2s = Parts(*(sb(first, f"W2_{part}", [P, K, D], F32R) for part in ("high", "low")))
            b1c = sb(first, "b1c", [P, K])
            b2r = sb(first, "b2r", [P, D])
            bgr = sb(first, "bgr", [P, G4 // PAIR, PAIR])
            s_w = sem(first, "s_w")
            s_w12 = sem(first, "s_w12")
            s_wx = sem(first, "s_wx")

            loads = [(W1s[:, :, :], W1.rearrange("(k p) c -> p k c", p=P), s_w12),
                     *((to, of, s_wx) for to, of in gate_columns(Wh, 0)),
                     (b1c[:, :], b1.rearrange("(m p) -> p m", p=P), s_w),
                     (b2r[:, :], b2.rearrange("(o d) -> o d", o=1).to_broadcast([P, D]), s_w)]
            for half in range(2):
                for n, (bank, slot) in enumerate(((0, 0), (0, 1), (1, 0), (1, 1))):
                    loads.append((bgr[:, 2 * half + bank, slot * HALF:(slot + 1) * HALF],
                                  bg[n][half * HALF:(half + 1) * HALF].rearrange("(o d) -> o d", o=1)
                                  .to_broadcast([P, HALF]), s_w))

            table_part(nc, x, src, dst, table, loads, W2, Wh, Wx, W2s, s_w12, s_wx, ident, src_cols, dst_cols, ranges,
                       sb, pb, sem, N, D, TILES, BLOCKS, TPP, TROWS)
            graph_part(nc, x, table, x1_rows, gate_rows, Wx, W1s, W2s, b1c, b2r, bgr, s_w, 16 * (2 + 8),
                       Wh, s_wh, gate_columns, ident, src_cols, dst_cols, ranges,
                       sb, pb, sem, D, K, BLOCKS, TILES, G4, HALF, PAIR)
        lstm_part(nc, x1_rows, gate_rows, y, Wh, s_wh, WH_LOADS, ident,
                  sb, pb, sem, D, K, KH, STEPS, G4, HALF, PAIR, MORE)


class Parts:

    def __init__(self, high, low):
        self.high, self.low = high, low


def hold(e, passed, sem, value):
    e.wait_ge(sem, value)
    e.sem_inc(passed, 1)


def rsqrt_on_vector(e, after_own, var, root, r, t, s_root, roots, s_ready):
    e.wait_ge(s_root, roots)
    after_own(e.reciprocal(r, root))
    after_own(e.tensor_tensor(t, r, r, ALU.mult))
    after_own(e.tensor_tensor(t, t, var, ALU.mult))
    after_own(e.tensor_scalar(t, t, -0.5, 1.5, ALU.mult, ALU.add))
    last = e.tensor_tensor(r, r, t, ALU.mult)
    if s_ready is None:
        after_own(last)
    else:
        last.then_inc(s_ready, 1)


def table_part(nc, x, src, dst, table, weight_loads, W2, Wh, Wx, W2s, s_w12, s_wx,
               ident, src_cols, dst_cols, ranges,
               sb, pb, sem, N, D, TILES, BLOCKS, TPP, TROWS):
    LB = LOAD_BLOCKS
    K = D // P
    GROUPS = BLOCKS // LB
    assert GROUPS * LB == BLOCKS and GROUPS % 2 == 0
    x_v = x.rearrange("(g j p) d -> g p j d", j=LB, p=LANES)
    table_v = table.rearrange("(g j p) d -> g p j d", j=LB, p=LANES)
    ETILE = LANES
    LAYER_2_AT, GATES_AT = 2, 4
    ON_VECTOR = 2
    QUAD = 4

    with ExitStack() as ctx:
        xin = sb(ctx, "xin", [P, 2, LB, D])
        xout = sb(ctx, "xout", [P, 2, LB, D])
        stats = sb(ctx, "stats", [P, LB, 6])
        mv = sb(ctx, "mv", [P, 2, LB, 2])
        ve = sb(ctx, "ve", [P, LB])
        root = sb(ctx, "root", [P, LB])
        rs = sb(ctx, "rs", [P, 2, LB])
        minus = sb(ctx, "minus", [P, 2, LB])
        W2_stage = sb(ctx, "W2_stage", [P, K, D])
        rt = sb(ctx, "rt", [P, LB])
        raw_i = sb(ctx, "raw_i", [TROWS, 2, TPP * ETILE], I32)
        raw_f = sb(ctx, "raw_f", [TROWS, 2, TPP * ETILE])
        tmin = sb(ctx, "tmin", [TROWS, TPP])
        tmax = sb(ctx, "tmax", [TROWS, TPP])
        tile_no = sb(ctx, "tile_no", [TROWS, TPP])
        tile_up = sb(ctx, "tile_up", [TROWS, TPP])
        block_at = sb(ctx, "block_at", [TROWS, BLOCKS])
        keys = sb(ctx, "keys", [TROWS, 2, TPP, BLOCKS])
        far = sb(ctx, "far", [TROWS, 2, BLOCKS])
        ends = sb(ctx, "ends", [BLOCKS, 2])
        row = sb(ctx, "row", [1, 6, BLOCKS])
        ones_row = sb(ctx, "ones_row", [1, BLOCKS])
        turned = [pb(ctx, f"turned{n}", [P, QUAD, TROWS]) for n in range(4)]
        far_t = pb(ctx, "far_t", [BLOCKS, 2, TROWS])
        ends_t = pb(ctx, "ends_t", [1, 2, BLOCKS])

        s_x = [sem(ctx, f"s_x{n}") for n in range(2)]
        s_out = [sem(ctx, f"s_out{n}") for n in range(2)]
        s_raw = sem(ctx, "s_raw")
        s_ident = sem(ctx, "s_ident")
        s_ids = sem(ctx, "s_ids")
        s_own = sem(ctx, "s_own")
        s_var = sem(ctx, "s_var")
        s_root = sem(ctx, "s_root")
        s_rs = sem(ctx, "s_rs")
        s_norm = sem(ctx, "s_norm")
        s_part = sem(ctx, "s_part")
        s_w_high = sem(ctx, "s_w_high")
        s_w_low = sem(ctx, "s_w_low")
        s_norm_a = sem(ctx, "s_norm_a")
        s_float = sem(ctx, "s_float")
        s_turn = sem(ctx, "s_turn")
        s_far = sem(ctx, "s_far")
        s_far_t = sem(ctx, "s_far_t")
        s_ends = sem(ctx, "s_ends")
        s_ends_t = sem(ctx, "s_ends_t")

        block = ctx.enter_context(nc.Block())

        @block.sync
        def _(e):
            e.dma_start(raw_i[:, 0, :], src.rearrange("(p n) -> p n", p=TROWS)).then_inc(s_raw, 16)
            e.dma_start(raw_i[:, 1, :], dst.rearrange("(p n) -> p n", p=TROWS)).then_inc(s_raw, 16)
            def normalised(g):
                e.wait_ge(s_norm, (g + 1) * ON_VECTOR)
                e.wait_ge(s_norm_a, (g + 1) * (LB - ON_VECTOR))

            all_weight_loads = [(W2_stage[:, :, :], W2.rearrange("(k p) c -> p k c", p=P), s_w12), *weight_loads]
            per_group = -(-len(all_weight_loads) // (GROUPS - 2))
            for g in range(GROUPS + 1):
                if g < GROUPS:
                    if g >= 2:
                        normalised(g - 2)
                    e.dma_start(xin[0:LANES, g % 2], x_v[g]).then_inc(s_x[g % 2], 16)
                with nc.allow_non_contiguous_dma(reason="small bias column"):
                    for to, of, loaded in all_weight_loads[max(g - 1, 0) * per_group:g * per_group]:
                        e.dma_start(to, of).then_inc(loaded, 16)
                if g >= 1:
                    normalised(g - 1)
                    e.dma_start(table_v[g - 1], xout[0:LANES, (g - 1) % 2]).then_inc(s_out[(g - 1) % 2], 16)
            for n in range(2):
                e.wait_ge(s_out[n], 16 * (GROUPS // 2))

        @block.gpsimd
        def _(e):
            e.memset(ident[:, :], 0.0).then_inc(s_ident, 1)
            e.wait_ge(s_ident, 1)
            e.affine_select(out=ident[:, :], in_=ident[:, :], compare_op=ALU.not_equal, fill=1.0,
                            base=0, pattern=[[-1, P]], channel_multiplier=1).then_inc(s_ident, 1)
            e.memset(src_cols[:, TILES:], 0).then_inc(s_ids, 1)
            e.memset(dst_cols[:, TILES:], -1.0).then_inc(s_ids, 1)
            e.iota(block_at[:, :], pattern=[[LANES, BLOCKS]], base=0, channel_multiplier=0,
                   allow_small_or_imprecise_dtypes=True).then_inc(s_ids, 1)
            e.iota(tile_no[:, :], pattern=[[1, TPP]], base=1, channel_multiplier=TPP,
                   allow_small_or_imprecise_dtypes=True).then_inc(s_ids, 1)
            e.wait_ge(s_w_high, 1)
            e.tensor_tensor(W2s.low[:, :, :], W2_stage[:, :, :], W2s.high[:, :, :].bitcast(F32),
                            ALU.subtract).then_inc(s_w_low, 1)
            for k in range(K):
                e.wait_ge(s_w_high, 1 + k + 1)
                e.tensor_tensor(Wx.low[:, k].rearrange("p a b s c -> p (a b s c)"),
                                Wh[:, k].rearrange("p a b s c -> p (a b s c)"),
                                Wx.high[:, k].rearrange("p a b s c -> p (a b s c)").bitcast(F32),
                                ALU.subtract).then_inc(s_w_low, 1)

        @block.scalar
        def _(e):
            for g in range(GROUPS):
                b = g % 2
                e.wait_ge(s_var, g + 1)
                e.activation(root[0:LANES, :], ve[0:LANES, :], ACT.Sqrt).then_inc(s_root, 1)
                if g >= 2:
                    e.wait_ge(s_out[b], 16 * (g // 2))
                for j in range(ON_VECTOR, LB):
                    e.activation(xout[0:LANES, b, j, :], xin[0:LANES, b, j, :], ACT.Identity,
                                 bias=minus[0:LANES, b, j:j + 1]).then_inc(s_part, 1)
                e.wait_ge(s_rs, g + 1)
                for j in range(ON_VECTOR, LB):
                    e.wait_ge(s_part, g * (LB - ON_VECTOR) + (j - ON_VECTOR + 1))
                    n = e.activation(xout[0:LANES, b, j, :], xout[0:LANES, b, j, :], ACT.Copy,
                                     scale=rs[0:LANES, b, j:j + 1])
                    n.then_inc(s_norm_a, 1)
                if g == LAYER_2_AT:
                    e.wait_ge(s_w12, 2 * 16)
                    e.activation(W2s.high[:, :, :], W2_stage[:, :, :], ACT.Copy).then_inc(s_w_high, 1)
                if 0 <= g - GATES_AT < K:
                    e.wait_ge(s_wx, 8 * 16)
                    k = g - GATES_AT
                    e.activation(Wx.high[:, k], Wh[:, k], ACT.Copy).then_inc(s_w_high, 1)

        @block.tensor
        def _(e):
            e.wait_ge(s_ident, 2)
            e.wait_ge(s_float, 1)
            for which in range(2):
                for j in range(TPP):
                    t = e.transpose(turned[2 * which + j // QUAD][0:ETILE, j % QUAD, :],
                                    raw_f[:, which, j * ETILE:(j + 1) * ETILE], ident[0:TROWS, 0:TROWS])
            t.then_inc(s_turn, 1)
            e.wait_ge(s_far, 1)
            for n in range(2):
                t = e.transpose(far_t[:, n, :], far[:, n, :], ident[0:TROWS, 0:TROWS])
            t.then_inc(s_far_t, 1)
            e.wait_ge(s_ends, 1)
            for n in range(2):
                t = e.transpose(ends_t[:, n, :], ends[:, n:n + 1], ident[0:BLOCKS, 0:BLOCKS])
            t.then_inc(s_ends_t, 1)

        @block.vector
        def _(e):
            own = [0]

            def after_own(ins):
                own[0] += 1
                ins.then_inc(s_own, 1)
                e.wait_ge(s_own, own[0])

            for g in range(GROUPS):
                b = g % 2
                e.wait_ge(s_x[b], 16 * (g // 2 + 1))
                for j in range(LB):
                    e.bn_stats(stats[0:LANES, j, :], xin[0:LANES, b, j, :]).then_inc(s_own, 1)
                own[0] += LB
                e.wait_ge(s_own, own[0])
                if g >= 2:
                    e.wait_ge(s_norm_a, (g - 1) * (LB - ON_VECTOR))
                for j in range(LB):
                    e.bn_aggr(mv[0:LANES, b, j, :], stats[0:LANES, j, :]).then_inc(s_own, 1)
                own[0] += LB
                e.wait_ge(s_own, own[0])
                after_own(e.tensor_scalar(minus[0:LANES, b, :], mv[0:LANES, b, :, 0], -1.0, None, ALU.mult))
                e.tensor_scalar_add(ve[0:LANES, :], mv[0:LANES, b, :, 1], EPS).then_inc(s_var, 1)
                e.wait_ge(s_var, g + 1)
                rsqrt_on_vector(e, after_own, ve[0:LANES, :], root[0:LANES, :], rs[0:LANES, b, :],
                                rt[0:LANES, :], s_root, g + 1, s_rs)
                e.wait_ge(s_rs, g + 1)
                if g >= 2:
                    e.wait_ge(s_out[b], 16 * (g // 2))
                for j in range(ON_VECTOR):
                    e.tensor_scalar(xout[0:LANES, b, j, :], xin[0:LANES, b, j, :], mv[0:LANES, b, j, 0:1],
                                    rs[0:LANES, b, j:j + 1], ALU.subtract, ALU.mult).then_inc(s_norm, 1)

            e.wait_ge(s_raw, 32)
            e.tensor_copy(raw_f[:, :, :], raw_i[:, :, :]).then_inc(s_float, 1)
            e.wait_ge(s_float, 1)
            dst_tiles = raw_f[:, 1, :].rearrange("p (j n) -> p j n", j=TPP)
            after_own(e.tensor_reduce(tmin[:, :], dst_tiles, AX_X, ALU.min))
            after_own(e.tensor_reduce(tmax[:, :], dst_tiles, AX_X, ALU.max))
            e.wait_ge(s_turn, 1)
            for which, cols in ((0, src_cols), (1, dst_cols)):
                by_tile = cols[0:ETILE, 0:TILES].rearrange("e (p j) -> e j p", j=TPP)
                for q in range(TPP // QUAD):
                    after_own(e.tensor_copy(by_tile[:, q * QUAD:(q + 1) * QUAD, :],
                                            turned[2 * which + q][0:ETILE, :, :]))

            e.wait_ge(s_ids, 4)
            after_own(e.tensor_scalar(tile_up[:, :], tile_no[:, :], -1.0, float(TILES + 1), ALU.mult, ALU.add))
            after_own(e.tensor_scalar(tmin[:, :], tmin[:, :], float(LANES), None, ALU.subtract))
            for n, number in enumerate((tile_no, tile_up)):
                for j in range(TPP):
                    after_own(e.tensor_scalar(keys[:, n, j, :], block_at[:, :], tmin[:, j:j + 1],
                                              number[:, j:j + 1], ALU.is_gt, ALU.mult))
                    after_own(e.scalar_tensor_tensor(out=keys[:, n, j, :], in0=block_at[:, :],
                                                     scalar=tmax[:, j:j + 1], in1=keys[:, n, j, :],
                                                     op0=ALU.is_le, op1=ALU.mult))
                r = e.tensor_reduce(far[:, n, :], keys[:, n].rearrange("p j b -> p b j"), AX_X, ALU.max)
                if n == 0:
                    after_own(r)
            r.then_inc(s_far, 1)
            e.wait_ge(s_far_t, 1)
            e.tensor_reduce(ends[:, :], far_t[:, :, :], AX_X, ALU.max).then_inc(s_ends, 1)
            e.wait_ge(s_ends_t, 1)
            after_own(e.tensor_copy(row[:, 0:2, :], ends_t[:, :, :]))
            end, low, count = row[:, 0, :], row[:, 2, :], row[:, 3, :]
            after_own(e.tensor_scalar(low, row[:, 1, :], -1.0, float(TILES), ALU.mult, ALU.add))
            after_own(e.tensor_tensor(count, end, low, ALU.subtract))
            groups, upto = row[:, 4, :], row[:, 5, :]
            after_own(e.tensor_scalar(count, count, (GROUP - 1) / 2, 1.0 / GROUP, ALU.add, ALU.mult))
            after_own(e.tensor_scalar_add(count, count, 1.5 * 2.0 ** 23))
            after_own(e.tensor_scalar(groups, count, 1.5 * 2.0 ** 23, float(LEAST_GROUPS), ALU.subtract, ALU.max))
            after_own(e.tensor_scalar(ranges[:, :, 1], groups, float(LEAST_GROUPS), None, ALU.subtract))
            after_own(e.memset(ones_row[:, :], 1.0))
            after_own(e.tensor_tensor_scan(upto, groups, ones_row[:, :], 0.0, ALU.add, ALU.mult))
            after_own(e.tensor_tensor(ranges[:, :, 0], upto, groups, ALU.subtract))
            after_own(e.memset(ranges[:, :, 3], 0))
            after_own(e.tensor_copy(ranges[:, :, 2], low))


def graph_part(nc, x, table, x1_rows, gate_rows, Wx, W1s, W2s, b1c, b2r, bgr, s_w, WEIGHTS_LOADED,
               Wh, s_wh, gate_columns, ident, src_cols, dst_cols, ranges,
               sb, pb, sem, D, K, BLOCKS, TILES, G4, HALF, PAIR):
    x_v = x.rearrange("(b p) d -> b p d", p=LANES)
    table_v = table.rearrange("(b p) d -> b p d", p=LANES)
    x1_v = x1_rows.rearrange("(b p) d -> b p d", p=LANES)
    gate_v = gate_rows.rearrange("(b p) d -> b p d", p=LANES)
    L = LANES
    BANKS = G4 // PAIR
    assert LEAST_GROUPS * GROUP == 18

    with ExitStack() as ctx:
        node_id = sb(ctx, "node_id", [P, L])
        idx = [sb(ctx, f"idx{n}", [P, GROUP], I32) for n in range(LEAST_GROUPS + 1)]
        rows = [sb(ctx, f"rows{j}", [P, D]) for j in range(GROUP)]
        high = [sb(ctx, f"high{j}", [P, D], F32R) for j in range(PARTS)]
        low_part = [sb(ctx, f"low_part{j}", [P, D], F32R) for j in range(PARTS)]
        onehot = [sb(ctx, f"onehot{j}", [P, L], F32R) for j in range(GROUP)]
        xt = sb(ctx, "xt", [P, D])
        hin = sb(ctx, "hin", [P, D])
        hinT = sb(ctx, "hinT", [P, K, L])
        h1T = Parts(*(sb(ctx, f"h1T_{part}", [P, K, L], F32R) for part in ("high", "low")))
        zT = Parts(*(sb(ctx, f"zT_{part}", [P, K, L], F32R) for part in ("high", "low")))
        between = sb(ctx, "between", [P, D])
        x1 = sb(ctx, "x1", [P, D])
        z = sb(ctx, "z", [P, D])
        gout = sb(ctx, "gout", [P, 2, 2, PAIR])
        stats = sb(ctx, "gstats", [P, 6])
        mv = sb(ctx, "gmv", [P, 2])
        ve = sb(ctx, "gve", [P, 1])
        root = sb(ctx, "groot", [P, 1])
        rs = sb(ctx, "grs", [P, 1])
        minus = sb(ctx, "gminus", [P, 1])
        rt = sb(ctx, "grt", [P, 1])
        between_T = between[:, 0:K * L].rearrange("p (k l) -> p k l", k=K)
        agg = pb(ctx, "agg", [P, D])
        turned = pb(ctx, "rows_turned", [P, K, L])
        mid = [pb(ctx, f"mid{n}", [P, K // 2, L]) for n in range(2)]
        late = pb(ctx, "late", [P, D])
        gps = [pb(ctx, f"gps{n}", [P, PAIR]) for n in range(2)]

        s_xt = sem(ctx, "s_xt")
        s_nt = sem(ctx, "s_nt")
        s_zero = sem(ctx, "s_zero")
        s_rows = [sem(ctx, f"s_rows{j}") for j in range(GROUP)]
        s_idx = sem(ctx, "s_idx")
        s_hot = sem(ctx, "s_hot")
        s_high = sem(ctx, "s_high")
        s_low = sem(ctx, "s_low")
        s_visit = sem(ctx, "s_visit")
        s_agg = sem(ctx, "s_agg")
        s_hin = sem(ctx, "s_hin")
        s_hin_t = sem(ctx, "s_hin_t")
        s_hinT = sem(ctx, "s_hinT")
        s_mid = [sem(ctx, f"s_mid{m}") for m in range(2)]
        s_relu = [sem(ctx, f"s_relu{m}") for m in range(2)]
        s_h1 = [sem(ctx, f"s_h1{m}") for m in range(2)]
        s_h1_low = sem(ctx, "s_h1_low")
        s_late = sem(ctx, "s_late")
        s_own = sem(ctx, "s_gown")
        s_passed = sem(ctx, "s_gpassed")
        s_x1 = sem(ctx, "s_x1")
        s_var = sem(ctx, "s_gvar")
        s_root = sem(ctx, "s_groot")
        s_rs = sem(ctx, "s_grs")
        s_less = sem(ctx, "s_less")
        s_z = sem(ctx, "s_z")
        s_z_t = sem(ctx, "s_z_t")
        s_zT = sem(ctx, "s_zT")
        s_zT_low = sem(ctx, "s_zT_low")
        s_gps = [sem(ctx, f"s_gps{n}") for n in range(BANKS)]
        s_gout = [sem(ctx, f"s_gout{n}") for n in range(BANKS)]
        s_x1_st = sem(ctx, "s_x1_st")
        s_g_st = [sem(ctx, f"s_g_st{n}") for n in range(2)]

        block = ctx.enter_context(nc.Block())

        def wait(e, semaphore, value):
            if not isinstance(value, int) or value > 0:
                e.wait_ge(semaphore, value)

        def all_iterations(e, one):
            one(0, True, False, False)
            one(1, True, True, False)
            one(2, True, True, True)
            with e.Fori(3, BLOCKS) as i:
                one(i, True, True, True)
            one(BLOCKS, False, True, True)
            one(BLOCKS + 1, False, False, True)

        def visits_of(e, i, tiles):
            if tiles:
                return block_visits(e, i)
            return (lambda first, last, *visits: None), (lambda *visits: None)

        def block_visits(e, b):
            _, (before, extra, low) = nc.values_load_multi_w_load_instructions(
                ranges[0:1, bass.ds(b, 1), 0:3].rearrange("o b n -> o (b n)"), engines=[e.engine],
                min_val=0, max_val=BLOCKS * TILES)
            extra = nc.s_assert_within(extra, 0, -(-TILES // GROUP),
                                       skip_runtime_bounds_check_because="the first part bounds it")

            def group(g, first, last, slab, visits):
                def column(j):
                    return nc.s_assert_within(
                        low + g * GROUP + j, 0, TILES + (LEAST_GROUPS - 1) * GROUP + j,
                        skip_runtime_bounds_check_because="a range ends at TILES, rounded up to the groups")

                for j in range(first, last):
                    for visit in visits:
                        visit(before + g, j, column, slab)

            def beyond(*visits):
                with e.If(extra > 0):
                    with e.Fori(0, extra) as g:
                        group(g + LEAST_GROUPS, 0, GROUP, LEAST_GROUPS, visits)

            def some(first, last, *visits):
                for n in range(LEAST_GROUPS):
                    begin, end = max(first, n * GROUP), min(last, (n + 1) * GROUP)
                    if begin < end:
                        group(n, begin - n * GROUP, end - n * GROUP, n, visits)
            return some, beyond

        @block.sync
        def _(e):
            def store_gates(b, half):
                for n in range(2):
                    e.wait_ge(s_gout[2 * half + n], b + 1)
                e.dma_start(gate_v[b][:, half * 2 * PAIR:(half + 1) * 2 * PAIR],
                            gout[0:L, half]).then_inc(s_g_st[half], 16)

            def one(i, tiles, layers, gates):
                if tiles:
                    wait(e, s_hin_t, i)
                    e.dma_start(hin[0:L, :], table_v[i]).then_inc(s_nt, 16)
                if layers:
                    wait(e, s_x1, i - 1)
                    e.dma_start(xt[0:L, :], x_v[i - 1]).then_inc(s_xt, 16)
                if gates:
                    store_gates(i - 2, 0)
                if layers:
                    e.wait_ge(s_x1, i)
                    e.dma_start(x1_v[i - 1], x1[0:L, :]).then_inc(s_x1_st, 16)
                if gates:
                    store_gates(i - 2, 1)
                if isinstance(i, int) and i == 0:
                    for dst_ap, src_ap in gate_columns(Wh, D):
                        e.dma_start(dst_ap, src_ap).then_inc(s_wh, 16)

            all_iterations(e, one)
            e.wait_ge(s_x1_st, 16 * BLOCKS)
            for half in range(2):
                e.wait_ge(s_g_st[half], 16 * BLOCKS)

        @block.gpsimd
        def _(e):
            def gather(q, j, column, slab):
                n = q * GROUP + j
                if j == 0:
                    if slab == LEAST_GROUPS:
                        e.wait_ge(s_low, n + GROUP)
                    else:
                        e.wait_ge(s_low, n + 1)
                    e.tensor_copy(idx[slab][0:L, :], src_cols[0:L, bass.ds(column(0), GROUP)]).then_inc(s_idx, 1)
                    hold(e, s_passed, s_idx, q + 1)
                else:
                    hold(e, s_passed, s_low, n + 1)
                e.indirect_dma_start(
                    out=rows[j][0:L, :], out_offset=None, in_=table[:, :],
                    in_offset=bass.IndirectOffsetOnAxis(ap=idx[slab][0:L, j:j + 1], axis=0),
                ).then_inc(s_rows[j], 16)

            with e.Fori(0, BLOCKS) as b:
                some, beyond = block_visits(e, b)
                some(0, LEAST_GROUPS * GROUP, gather)
                beyond(gather)

        @block.scalar
        def _(e):
            def high_part(q, j, column, slab):
                n = q * GROUP + j
                e.wait_ge(s_rows[j], (q + 1) * 16)
                e.wait_ge(s_visit, n + 1 + GROUP - PARTS)
                e.activation(high[j % PARTS][0:L, :], rows[j][0:L, :], ACT.Copy).then_inc(s_high, 1)

            def one(i, tiles, layers, gates):
                some, beyond = visits_of(e, i, tiles)
                some(0, 3, high_part)
                if layers:
                    e.wait_ge(s_hin_t, i)
                    e.activation(hinT[:, :, :], turned[:, :, :], ACT.Copy).then_inc(s_hinT, 1)
                some(3, 6, high_part)
                if layers:
                    for half in range(2):
                        e.wait_ge(s_mid[half], i)
                        for m in range(2 * half, 2 * half + 2):
                            e.activation(between_T[:, m, :], mid[half][:, m % 2, :], ACT.Relu,
                                         bias=b1c[:, m:m + 1]).then_inc(s_relu[half], 1)
                        e.wait_ge(s_relu[half], i * 2)
                        of = slice(2 * half, 2 * half + 2)
                        e.activation(h1T.high[:, of, :], between_T[:, of, :], ACT.Copy).then_inc(s_h1[half], 1)
                some(6, 9, high_part)
                if layers:
                    e.wait_ge(s_var, i)
                    e.activation(root[0:L, :], ve[0:L, :], ACT.Sqrt).then_inc(s_root, 1)
                    wait(e, s_z_t, i - 1)
                    e.activation(z[0:L, :], x1[0:L, :], ACT.Identity, bias=minus[0:L, :]).then_inc(s_less, 1)
                some(9, 12, high_part)
                if layers:
                    e.wait_ge(s_less, i)
                    e.wait_ge(s_rs, i)
                    e.activation(z[0:L, :], z[0:L, :], ACT.Copy, scale=rs[0:L, :]).then_inc(s_z, 1)
                some(12, 15, high_part)
                if layers:
                    e.wait_ge(s_z_t, i)
                    e.activation(zT.high[:, :, :], turned[:, :, :], ACT.Copy).then_inc(s_zT, 1)
                some(15, 18, high_part)
                beyond(high_part)

            e.wait_ge(s_w, WEIGHTS_LOADED)
            all_iterations(e, one)

        @block.tensor
        def _(e):
            def visit(q, j, column, slab):
                n = q * GROUP + j
                e.wait_ge(s_hot, n + 1)
                e.wait_ge(s_low, n + 1 + GROUP)
                begins = slab == 0 and j == 0
                for part in (high, low_part):
                    m = e.matmul(agg[0:L, :], onehot[j][0:L, :], part[j % PARTS][0:L, :],
                                 start=begins, stop=(part is low_part), skip_group_check=True)
                    begins = False
                m.then_inc(s_visit, 1)

            def turn(rows_of):
                for k in range(K):
                    t = e.transpose(turned[:, k, :], rows_of[0:L, k * P:(k + 1) * P], ident[0:L, 0:L])
                return t

            def bank_products(n, state, weights, begins=False, ends=False):
                products = []
                for k in range(K):
                    products.append(e.matmul(
                        gps[n % 2][0:L, :], state[:, k, :],
                        weights[:, k, n // 2, n % 2].rearrange("p s c -> p (s c)"),
                        start=(begins and k == 0), stop=(ends and k == K - 1), skip_group_check=True))
                return products

            def gate_high(b, n, agg_done=False):
                if n >= 2:
                    e.wait_ge(s_gout[n - 2], b + 1)
                else:
                    wait(e, s_gout[n + 2], b)
                products = bank_products(n, zT.high, Wx.high, begins=True)
                if agg_done:
                    products[0].then_inc(s_agg, 1)
                bank_products(n, zT.high, Wx.low)

            def gate_low(b, n):
                e.wait_ge(s_zT_low, b + 1)
                bank_products(n, zT.low, Wx.high, ends=True)[-1].then_inc(s_gps[n], 1)

            def one(i, tiles, layers, gates):
                some, beyond = visits_of(e, i, tiles)
                wait(e, s_hin, i if tiles or layers else 0)
                if layers:
                    wait(e, s_zT_low, i - 1)
                    turn(hin).then_inc(s_hin_t, 1)
                some(0, 3, visit)
                if layers:
                    e.wait_ge(s_hinT, i)
                    for m in range(K):
                        for k in range(K):
                            mm = e.matmul(mid[m // 2][:, m % 2, :], W1s[:, k, m * P:(m + 1) * P], hinT[:, k, :],
                                          start=(k == 0), stop=(k == K - 1))
                        if m % 2:
                            mm.then_inc(s_mid[m // 2], 1)
                some(3, 6, visit)
                if layers:
                    for k in range(K):
                        if k % 2 == 0:
                            e.wait_ge(s_h1[k // 2], i)
                        for weights in (W2s.high, W2s.low):
                            e.matmul(late[0:L, :], h1T.high[:, k, :], weights[:, k, :],
                                     start=(k == 0 and weights is W2s.high), stop=False, skip_group_check=True)
                    e.wait_ge(s_h1_low, i)
                    for k in range(K):
                        mm = e.matmul(late[0:L, :], h1T.low[:, k, :], W2s.high[:, k, :], start=False,
                                      stop=(k == K - 1), skip_group_check=True)
                    mm.then_inc(s_late, 1)
                if gates:
                    gate_high(i - 2, 2)
                    gate_low(i - 2, 2)
                some(6, 9, visit)
                if gates:
                    gate_high(i - 2, 3)
                some(9, 12, visit)
                if layers:
                    e.wait_ge(s_z, i)
                    e.wait_ge(s_hinT, i)
                    turn(z).then_inc(s_z_t, 1)
                if gates:
                    gate_low(i - 2, 3)
                some(12, 15, visit)
                if layers:
                    e.wait_ge(s_zT, i)
                    gate_high(i - 1, 0)
                    gate_low(i - 1, 0)
                some(15, 18, visit)
                beyond(visit)
                if layers:
                    gate_high(i - 1, 1, agg_done=tiles)
                    gate_low(i - 1, 1)
                elif tiles:
                    e.drain().then_inc(s_agg, 1)

            e.wait_ge(s_w, WEIGHTS_LOADED)
            e.sem_inc(s_visit, GROUP)
            all_iterations(e, one)

        @block.vector
        def _(e):
            OWN = 12

            def one_hot(q, j, column, slab):
                e.wait_ge(s_visit, q * GROUP + j + 1)
                e.tensor_scalar(onehot[j][0:L, :], node_id[0:L, :], dst_cols[0:L, bass.ds(column(j), 1)],
                                None, ALU.is_equal).then_inc(s_hot, 1)

            def low_of_rows(q, j, column, slab):
                e.wait_ge(s_high, q * GROUP + j + 1)
                e.tensor_tensor(low_part[j % PARTS][0:L, :], rows[j][0:L, :],
                                high[j % PARTS][0:L, :].bitcast(F32), ALU.subtract).then_inc(s_low, 1)

            def low_of_turned(parts, s_high_part, i, s_low_part):
                e.wait_ge(s_high_part, i)
                e.tensor_tensor(parts.low[:, :, :], turned[:, :, :], parts.high[:, :, :].bitcast(F32),
                                ALU.subtract).then_inc(s_low_part, 1)

            def gate_biases(b, n):
                if n % 2 == 0:
                    wait(e, s_g_st[n // 2], b * 16)
                e.wait_ge(s_gps[n], b + 1)
                e.tensor_tensor(gout[0:L, n // 2, n % 2, :], gps[n % 2][0:L, :], bgr[0:L, n, :],
                                ALU.add).then_inc(s_gout[n], 1)

            def one(i, tiles, layers, gates):
                own = [i * OWN]

                def after_own(ins):
                    own[0] = own[0] + 1
                    ins.then_inc(s_own, 1)
                    e.wait_ge(s_own, own[0])

                some, beyond = visits_of(e, i, tiles)
                some(0, 3, one_hot)
                if layers:
                    e.wait_ge(s_agg, i)
                    e.wait_ge(s_nt, i * 16)
                    e.tensor_tensor(hin[0:L, :], agg[0:L, :], hin[0:L, :], ALU.add).then_inc(s_hin, 1)
                some(0, 3, low_of_rows)
                if gates:
                    gate_biases(i - 2, 0)
                some(3, 6, one_hot)
                if gates:
                    gate_biases(i - 2, 1)
                some(3, 6, low_of_rows)
                some(6, 12, one_hot)
                if layers:
                    for half in range(2):
                        e.wait_ge(s_h1[half], i)
                    e.tensor_tensor(h1T.low[:, :, :], between_T[:, :, :], h1T.high[:, :, :].bitcast(F32),
                                    ALU.subtract).then_inc(s_h1_low, 1)
                some(6, 9, low_of_rows)
                some(12, 15, one_hot)
                if layers:
                    e.wait_ge(s_late, i)
                    after_own(e.tensor_tensor(between[0:L, :], late[0:L, :], b2r[0:L, :], ALU.add))
                    e.wait_ge(s_xt, i * 16)
                    wait(e, s_x1_st, (i - 1) * 16)
                    e.scalar_tensor_tensor(out=x1[0:L, :], in0=between[0:L, :], scalar=0.0, in1=xt[0:L, :],
                                           op0=ALU.max, op1=ALU.add).then_inc(s_x1, 1)
                    e.wait_ge(s_x1, i)
                    e.bn_stats(stats[0:L, :], x1[0:L, :]).then_inc(s_own, 1)
                    own[0] = own[0] + 1
                    hold(e, s_passed, s_own, own[0])
                    after_own(e.bn_aggr(mv[0:L, :], stats[0:L, :]))
                    after_own(e.tensor_scalar(minus[0:L, :], mv[0:L, 0:1], -1.0, None, ALU.mult))
                    e.tensor_scalar_add(ve[0:L, :], mv[0:L, 1:2], EPS).then_inc(s_var, 1)
                if gates:
                    gate_biases(i - 2, 2)
                if layers:
                    e.wait_ge(s_var, i)
                    rsqrt_on_vector(e, after_own, ve[0:L, :], root[0:L, :], rs[0:L, :], rt[0:L, :],
                                    s_root, i, s_rs)
                some(9, 12, low_of_rows)
                some(12, 15, low_of_rows)
                if gates:
                    gate_biases(i - 2, 3)
                some(15, 18, one_hot)
                if layers:
                    low_of_turned(zT, s_zT, i, s_zT_low)
                some(15, 18, low_of_rows)
                beyond(one_hot, low_of_rows)
                if tiles:
                    after_own(e.tensor_scalar_add(node_id[0:L, :], node_id[0:L, :], float(L)))
                e.sem_inc(s_own, OWN - (8 if layers else 0) - (1 if tiles else 0))

            e.sem_inc(s_low, GROUP)
            e.wait_ge(s_w, WEIGHTS_LOADED)
            e.memset(node_id[0:L, :], 0.0).then_inc(s_zero, 1)
            e.memset(x1[0:L, 0:L], 1.0).then_inc(s_zero, 1)
            e.wait_ge(s_zero, 2)
            e.tensor_tensor_scan(node_id[0:L, :], x1[0:L, 0:L], x1[0:L, 0:L], -1.0, ALU.add,
                                 ALU.mult).then_inc(s_zero, 1)
            e.wait_ge(s_zero, 3)
            all_iterations(e, one)


def lstm_part(nc, x1_rows, gate_rows, y, Wh, s_wh, WH_LOADS, ident,
              sb, pb, sem, D, K, KH, STEPS, G4, HALF, PAIR, MORE):
    L = LANES
    AHEAD = 2
    gates_v = gate_rows.rearrange("(c t) g -> t c g", t=STEPS)
    x1_v = x1_rows.rearrange("(c t) d -> t c d", t=STEPS)
    y_v = y.rearrange("(c t) d -> t c d", t=STEPS)

    with ExitStack() as ctx:
        W_high = sb(ctx, "W_high", [P, K, 2, 2, 2, HALF], F32R)
        W_low = sb(ctx, "W_low", [P, K, 2, 2, 2, HALF], F32R)
        h_high = sb(ctx, "h_high", [P, K, L], F32R)
        h_low = sb(ctx, "h_low", [P, K, L], F32R)
        xg = [sb(ctx, f"xg{n}", [P, 2, 2, PAIR]) for n in range(2)]
        total = sb(ctx, "total", [P, 2, 2, PAIR])
        gate = sb(ctx, "gate", [P, 2, 2, 2, HALF])
        c = sb(ctx, "c", [P, 2, HALF])
        fc = sb(ctx, "fc", [P, 2, HALF])
        ic = sb(ctx, "ic", [P, 2, HALF])
        tc = sb(ctx, "tc", [P, 2, HALF])
        h = [sb(ctx, f"h{n}", [P, 2, HALF]) for n in range(2)]
        decay = sb(ctx, "decay", [P, 2, HALF])
        x1 = [sb(ctx, f"lx1{n}", [P, D]) for n in range(2)]
        out = [sb(ctx, f"out{n}", [P, D]) for n in range(2)]
        c_start = sb(ctx, "c_start", [P, K, L])
        h_start = sb(ctx, "h_start", [P, K, L])
        gap = sb(ctx, "gap", [P, K, L])
        h_gap = sb(ctx, "h_gap", [P, K, L])
        change = sb(ctx, "change", [P, K, L])
        tc_start = sb(ctx, "tc_start", [P, K, L])
        most = sb(ctx, "most", [P, 4])
        worst = sb(ctx, "worst", [P, 1])
        worst1 = sb(ctx, "worst1", [1, 2])
        apart = sb(ctx, "apart", [1, 1], I32)

        acc = [pb(ctx, f"acc{n}", [P, PAIR]) for n in range(4)]
        hturn = [pb(ctx, f"hturn{n}", [P, KH, L]) for n in range(2)]
        back = pb(ctx, "back", [P, D])
        worst_t = pb(ctx, "worst_t", [1, P])
        c_end_t, decay_t, out_gate_t = (acc[n][:, 0:K * L].rearrange("p (k l) -> p k l", k=K) for n in range(3))

        s_acc = [sem(ctx, f"s_acc{n}") for n in range(4)]
        s_sum = [sem(ctx, f"s_sum{n}") for n in range(4)]
        s_sum_cell = [sem(ctx, f"s_sum_cell{n}") for n in range(2)]
        s_fi = [sem(ctx, f"s_fi{n}") for n in range(2)]
        s_ct = [sem(ctx, f"s_ct{n}") for n in range(2)]
        s_o = [sem(ctx, f"s_o{n}") for n in range(2)]
        s_prod = [sem(ctx, f"s_prod{n}") for n in range(2)]
        s_c = [sem(ctx, f"s_c{n}") for n in range(2)]
        s_tc = [sem(ctx, f"s_tc{n}") for n in range(2)]
        s_h = [sem(ctx, f"s_h{n}") for n in range(2)]
        s_turn = [sem(ctx, f"s_lturn{n}") for n in range(2)]
        s_high = [sem(ctx, f"s_hhigh{n}") for n in range(2)]
        s_low = [sem(ctx, f"s_hlow{n}") for n in range(2)]
        s_decay = [sem(ctx, f"s_decay{n}") for n in range(2)]
        s_xg = [sem(ctx, f"s_xg{n}") for n in range(2)]
        s_x1 = [sem(ctx, f"s_lx1{n}") for n in range(2)]
        s_out = sem(ctx, "s_lout")
        s_y = [sem(ctx, f"s_y{n}") for n in range(2)]
        s_init = sem(ctx, "s_init")
        s_own = sem(ctx, "s_lown")
        s_ends = sem(ctx, "s_lends")
        s_cs = sem(ctx, "s_cs")
        s_tcs = sem(ctx, "s_tcs")
        s_back = sem(ctx, "s_back")
        s_begin = sem(ctx, "s_begin")
        s_fresh = sem(ctx, "s_fresh")
        s_worst = sem(ctx, "s_worst")
        s_worst_t = sem(ctx, "s_worst_t")
        s_apart = sem(ctx, "s_apart")
        s_passed = sem(ctx, "s_lpassed")

        block = ctx.enter_context(nc.Block())

        def steps_of_round(e, r, step):
            base = r * STEPS + AHEAD + 1
            step(0, 0, base, True, False)
            with e.Fori(0, STEPS // 2 - 1) as i:
                step(i * 2 + 1, 1, base + i * 2 + 1, False, False)
                step(i * 2 + 2, 0, base + i * 2 + 2, False, False)
            step(STEPS - 1, 1, base + (STEPS - 1), False, True)

        def all_rounds(e, one_round, signal_anyway=None):
            with e.Fori(0, ROUGH) as r:
                one_round(r, False, False, r)
            for f in range(FINE - 1):
                one_round(ROUGH + f, True, False, f)
            one_round(ROUGH + FINE - 1, True, True, FINE - 1)

            def not_met(checks):
                hold(e, s_passed, s_apart, checks)
                return e.value_load(apart[0:1, 0:1], min_val=0, max_val=1)

            with e.If(not_met(FINE) == 1):
                with e.Fori(0, MORE) as m:
                    with e.If(not_met(m + FINE) == 1):
                        one_round(m + (ROUGH + FINE), True, True, m + FINE)
                    with e.Else():
                        if signal_anyway is not None:
                            e.sem_inc(signal_anyway, 1)

        @block.sync
        def _(e):
            for n in range(2):
                e.sem_inc(s_y[n], 16)

            def store(s, par, now):
                e.wait_ge(s_out, now)
                e.dma_start(y_v[s], out[par][0:L, :]).then_inc(s_y[par], 16)

            def one_round(r, fine, writes, checked):
                def step(s, par, now, first, last):
                    e.wait_ge(s_sum[3], now - 2)
                    e.dma_start(xg[par][0:L].rearrange("c a b g -> c (a b g)"), gates_v[s]).then_inc(s_xg[par], 16)
                    if writes:
                        e.wait_ge(s_out, now - 2)
                        e.dma_start(x1[par][0:L, :], x1_v[s]).then_inc(s_x1[par], 16)
                        if not first:
                            store(s - 1, 1 - par, now - 1)
                        if last:
                            store(s, par, now)
                steps_of_round(e, r, step)
                if writes:
                    written = (r - (ROUGH + FINE - 1) + 1) * (STEPS // 2)
                    for n in range(2):
                        hold(e, s_passed, s_y[n], written * 16 + 16)
            all_rounds(e, one_round)

        @block.gpsimd
        def _(e):
            for s in s_decay:
                e.sem_inc(s, AHEAD)
            e.sem_inc(s_out, AHEAD + (ROUGH + FINE - 1) * STEPS)

            def one_round(r, fine, writes, checked):
                e.wait_ge(s_fresh, r + 1 + K)
                def step(s, par, now, first, last):
                    for half in range(2):
                        e.wait_ge(s_fi[half], now)
                        e.wait_ge(s_decay[half], now - 1)
                        e.tensor_tensor(decay[0:L, half], decay[0:L, half], gate[0:L, half, 0, 0],
                                        ALU.mult).then_inc(s_decay[half], 1)
                    if writes:
                        n = now - (AHEAD + 1) - (ROUGH + FINE - 1) * STEPS
                        e.wait_ge(s_x1[par], (n - par) * 8 + 16)
                        e.wait_ge(s_y[par], (n - par) * 8 + 16)
                        for half in range(2):
                            e.wait_ge(s_h[half], now)
                        e.tensor_tensor(out[par][0:L, :], h[par][0:L].rearrange("c a u -> c (a u)"),
                                        x1[par][0:L, :], ALU.add).then_inc(s_out, 1)
                steps_of_round(e, r, step)
            all_rounds(e, one_round)

        @block.scalar
        def _(e):
            for s in (*s_fi, *s_ct, *s_o, *s_tc, *s_high):
                e.sem_inc(s, AHEAD)
            e.wait_ge(s_wh, 16 * WH_LOADS)
            e.activation(W_high[:, 0:1, 0, 0, 0, 0:2], Wh[:, 0:1, 0, 0, 0, 0:2], ACT.Sigmoid).then_inc(s_init, 1)
            e.wait_ge(s_init, 1)
            for k in range(K):
                e.activation(W_high[:, k], Wh[:, k], ACT.Copy).then_inc(s_init, 1)

            def one_round(r, fine, writes, checked):
                def take_turned(half, now):
                    e.wait_ge(s_turn[half], now)
                    e.activation(h_high[:, half * KH:(half + 1) * KH, :], hturn[half][:, :, :],
                                 ACT.Copy).then_inc(s_high[half], 1)

                def step(s, par, now, first, last):
                    if not first:
                        take_turned(1, now - 1)
                    else:
                        e.wait_ge(s_begin, r + 1)

                    def before_function(half, bank):
                        n = 2 * half + bank
                        if fine or n == 3:
                            e.wait_ge(s_sum_cell[half] if bank else s_sum[n], now)
                            return total[0:L, half, bank]
                        e.wait_ge(s_acc[n], now)
                        return acc[n][0:L, :]

                    def forget_input(half):
                        gates = before_function(half, 0)
                        e.wait_ge(s_decay[half], now - 1)
                        e.activation(gate[0:L, half, 0].rearrange("c s u -> c (s u)"), gates,
                                     ACT.Sigmoid).then_inc(s_fi[half], 1)

                    def cell_output(half):
                        gates = before_function(half, 1)
                        e.activation(gate[0:L, half, 1, 0], gates[:, 0:HALF], ACT.Tanh).then_inc(s_ct[half], 1)
                        if fine or half == 1:
                            e.wait_ge(s_sum[2 * half + 1], now)
                        e.activation(gate[0:L, half, 1, 1], gates[:, HALF:PAIR],
                                     ACT.Sigmoid).then_inc(s_o[half], 1)

                    def new_cell(half):
                        e.wait_ge(s_c[half], now)
                        e.activation(tc[0:L, half], c[0:L, half], ACT.Tanh).then_inc(s_tc[half], 1)

                    forget_input(0)
                    cell_output(0)
                    if fine:
                        new_cell(0)
                        take_turned(0, now)
                        forget_input(1)
                        cell_output(1)
                    else:
                        forget_input(1)
                        new_cell(0)
                        cell_output(1)
                        take_turned(0, now)
                    new_cell(1)
                    if last:
                        take_turned(1, now)
                steps_of_round(e, r, step)
                e.wait_ge(s_cs, r + 1)
                e.activation(tc_start[:, :, :], c_start[:, :, :], ACT.Tanh).then_inc(s_tcs, 1)
            all_rounds(e, one_round)

        @block.tensor
        def _(e):
            for s in (*s_acc, *s_turn):
                e.sem_inc(s, AHEAD)
            e.wait_ge(s_init, 1 + K)

            def one_round(r, fine, writes, checked):
                def products(n, ks, pairs, begins):
                    for k in ks:
                        for state, weights in pairs:
                            m = e.matmul(acc[n][0:L, :], state[:, k, :],
                                         weights[:, k, n // 2, n % 2].rearrange("p s c -> p (s c)"),
                                         start=begins, stop=(k == K - 1), skip_group_check=True)
                            begins = False
                    return m

                FIRST, SECOND = range(KH), range(KH, K)
                ROUNDED = [(h_high, W_high)]
                OF_HIGH = [(h_high, W_high), (h_high, W_low)]
                OF_LOW = [(h_low, W_high)]

                def turn(half, par, now):
                    e.wait_ge(s_h[half], now)
                    for k in range(KH):
                        t = e.transpose(hturn[half][:, k, :], h[par][0:L, half, k * P:(k + 1) * P],
                                        ident[0:L, 0:L])
                    t.then_inc(s_turn[half], 1)

                def add_rows(n, par, now):
                    half, bank = n // 2, n % 2
                    if n == 0:
                        count = now - (AHEAD + 1)
                        e.wait_ge(s_xg[par], (count - par) * 8 + 16)
                    e.wait_ge(s_o[half] if bank else s_fi[half], now - 1)
                    e.matmul(acc[n][0:L, :], ident[0:L, 0:L], xg[par][0:L, half, bank], start=True, stop=False,
                             skip_group_check=True)

                def rough_step(s, par, now, first, last):
                    if first:
                        e.wait_ge(s_begin, r + 1)
                    for n in range(2):
                        add_rows(n, par, now)
                    if not first:
                        turn(0, 1 - par, now - 1)
                    add_rows(2, par, now)
                    if not first:
                        e.wait_ge(s_high[0], now - 1)
                    e.wait_ge(s_sum[3], now - 1)
                    for n in range(4):
                        products(n, FIRST, ROUNDED, begins=(n == 3))
                        if n == 1 and not first:
                            turn(1, 1 - par, now - 1)
                    if not first:
                        e.wait_ge(s_high[1], now - 1)
                    for n in range(4):
                        products(n, SECOND, ROUNDED, False).then_inc(s_acc[n], 1)
                    if last:
                        for half in range(2):
                            turn(half, par, now)

                def fine_step(s, par, now, first, last):
                    if first:
                        e.wait_ge(s_begin, r + 1)
                    else:
                        e.wait_ge(s_high[0], now - 1)
                    for n in range(2):
                        e.wait_ge(s_sum[n], now - 1)
                        products(n, FIRST, OF_HIGH, True)
                    e.wait_ge(s_low[0], now - 1)
                    for n in range(2):
                        products(n, FIRST, OF_LOW, False)
                    e.wait_ge(s_sum[2], now - 1)
                    products(2, FIRST, OF_HIGH, True)
                    if not first:
                        turn(1, 1 - par, now - 1)
                    products(2, FIRST, OF_LOW, False)
                    for n in range(2):
                        if not first and n == 0:
                            e.wait_ge(s_high[1], now - 1)
                        products(n, SECOND, OF_HIGH, False)
                        if n == 0:
                            e.wait_ge(s_low[1], now - 1)
                        products(n, SECOND, OF_LOW, False).then_inc(s_acc[n], 1)
                    e.wait_ge(s_sum[3], now - 1)
                    products(3, FIRST, OF_HIGH + OF_LOW, True)
                    products(2, SECOND, OF_HIGH + OF_LOW, False).then_inc(s_acc[2], 1)
                    products(3, SECOND[:1], OF_HIGH, False)
                    turn(0, par, now)
                    products(3, SECOND[1:], OF_HIGH, False)
                    products(3, SECOND, OF_LOW, False).then_inc(s_acc[3], 1)
                    if last:
                        turn(1, par, now)

                step = fine_step if fine else rough_step
                steps_of_round(e, r, step)

                now = (r + 1) * STEPS + AHEAD
                for half in range(2):
                    e.wait_ge(s_c[half], now)
                    e.wait_ge(s_decay[half], now)
                    e.wait_ge(s_o[half], now)
                for n in range(4):
                    if fine or n == 3:
                        e.wait_ge(s_sum[n], now)
                if not fine:
                    for half in range(2):
                        e.wait_ge(s_fi[half], now)
                for to, of in ((c_end_t, c), (decay_t, decay), (out_gate_t, gate[:, :, 1, 1])):
                    for k in range(K):
                        u = (k % KH) * P
                        t = e.transpose(to[:, k, :], of[0:L, k // KH, u:u + P], ident[0:L, 0:L])
                t.then_inc(s_ends, 1)
                if fine:
                    e.wait_ge(s_worst, checked + 1)
                    e.transpose(worst_t[:, :], worst[:, :], ident[:, :]).then_inc(s_worst_t, 1)
                e.wait_ge(s_cs, r + 1)
                for k in range(K):
                    t = e.transpose(back[0:L, k * P:(k + 1) * P], c_start[:, k, :], ident[:, :])
                t.then_inc(s_back, 1)
            all_rounds(e, one_round)

        @block.vector
        def _(e):
            for s in (*s_sum, *s_sum_cell, *s_c, *s_h, *s_low):
                e.sem_inc(s, AHEAD)
            for s in s_prod:
                e.sem_inc(s, 2 * AHEAD)
            clear = (c, c_start, h_start, gap, h_gap, change)
            for t in clear:
                e.memset(t[:, :, :], 0.0).then_inc(s_own, 1)
            e.memset(decay[:, :, :], 1.0).then_inc(s_fresh, 1)
            e.wait_ge(s_own, len(clear))
            e.tensor_copy(h_high[:, :, :], h_start[:, :, :]).then_inc(s_begin, 1)
            for k in range(K):
                e.wait_ge(s_init, 2 + k)
                e.tensor_tensor(W_low[:, k].rearrange("p a b s c -> p (a b s c)"),
                                Wh[:, k].rearrange("p a b s c -> p (a b s c)"),
                                W_high[:, k].rearrange("p a b s c -> p (a b s c)").bitcast(F32),
                                ALU.subtract).then_inc(s_fresh, 1)
            CLEARED = len(clear)
            ROUGH_OWN, FINE_OWN = 12, 24

            def one_round(r, fine, writes, checked):
                def step(s, par, now, first, last):
                    count = now - (AHEAD + 1)
                    def add_inputs(n):
                        half, bank = n // 2, n % 2
                        e.wait_ge(s_acc[n], now)
                        if n == (0 if fine else 3):
                            e.wait_ge(s_xg[par], (count - par) * 8 + 16)
                        if bank == 0:
                            e.wait_ge(s_fi[half], now - 1)
                        else:
                            e.wait_ge(s_o[half], now - 1)
                        pieces = [(0, PAIR, s_sum[n])]
                        if bank == 1:
                            pieces = [(0, HALF, s_sum_cell[half]), (HALF, PAIR, s_sum[n])]
                        for begin, end, summed in pieces:
                            e.tensor_tensor(total[0:L, half, bank, begin:end], acc[n][0:L, begin:end],
                                            xg[par][0:L, half, bank, begin:end], ALU.add).then_inc(summed, 1)

                    def low_part(half, now):
                        e.wait_ge(s_high[half], now)
                        of = slice(half * KH, (half + 1) * KH)
                        e.tensor_tensor(h_low[:, of, :], hturn[half][:, :, :], h_high[:, of, :].bitcast(F32),
                                        ALU.subtract).then_inc(s_low[half], 1)

                    def forgotten(half):
                        e.wait_ge(s_fi[half], now)
                        e.tensor_tensor(fc[0:L, half], gate[0:L, half, 0, 0], c[0:L, half],
                                        ALU.mult).then_inc(s_prod[half], 1)

                    def new_cell(half):
                        e.wait_ge(s_ct[half], now)
                        e.tensor_tensor(ic[0:L, half], gate[0:L, half, 0, 1], gate[0:L, half, 1, 0],
                                        ALU.mult).then_inc(s_prod[half], 1)
                        e.wait_ge(s_prod[half], now * 2)
                        e.tensor_tensor(c[0:L, half], fc[0:L, half], ic[0:L, half],
                                        ALU.add).then_inc(s_c[half], 1)

                    def new_h(half):
                        e.wait_ge(s_o[half], now)
                        e.wait_ge(s_tc[half], now)
                        if writes and half == 0:
                            e.wait_ge(s_out, now - 1)
                        e.tensor_tensor(h[par][0:L, half], gate[0:L, half, 1, 1], tc[0:L, half],
                                        ALU.mult).then_inc(s_h[half], 1)

                    if fine:
                        if not first:
                            low_part(1, now - 1)
                        add_inputs(0)
                        add_inputs(1)
                        forgotten(0)
                        new_cell(0)
                        new_h(0)
                        add_inputs(2)
                        add_inputs(3)
                        low_part(0, now)
                        forgotten(1)
                    else:
                        forgotten(0)
                        new_cell(0)
                        add_inputs(3)
                        new_h(0)
                        forgotten(1)
                    new_cell(1)
                    new_h(1)
                    if last and fine:
                        low_part(1, now)
                steps_of_round(e, r, step)
                if not fine:
                    for n in range(3):
                        e.sem_inc(s_sum[n], STEPS)
                    e.sem_inc(s_sum_cell[0], STEPS)
                    for half in range(2):
                        e.sem_inc(s_low[half], STEPS)

                own = [(r - ROUGH) * FINE_OWN + ROUGH * ROUGH_OWN + CLEARED if fine
                       else r * ROUGH_OWN + CLEARED]

                def after_own(ins):
                    own[0] = own[0] + 1
                    ins.then_inc(s_own, 1)
                    e.wait_ge(s_own, own[0])

                signals = 0
                e.wait_ge(s_ends, r + 1)
                after_own(e.tensor_tensor(gap[:, :, 1:], c_end_t[:, :, 0:L - 1], c_start[:, :, 1:], ALU.subtract))
                signals += 1
                if fine:
                    for half in range(2):
                        of = slice(half * KH, (half + 1) * KH)
                        e.wait_ge(s_turn[half], (r + 1) * STEPS + AHEAD)
                        after_own(e.tensor_tensor(h_gap[:, of, 1:], hturn[half][:, :, 0:L - 1],
                                                  h_start[:, of, 1:], ALU.subtract))
                    for n, (g, op) in enumerate(((gap, ALU.max), (h_gap, ALU.max), (gap, ALU.min), (h_gap, ALU.min))):
                        after_own(e.tensor_reduce(most[:, n:n + 1], g[:, :, :].rearrange("p k l -> p (k l)"),
                                                  AX_X, op))
                    after_own(e.tensor_scalar(most[:, 2:4], most[:, 2:4], -1.0, None, ALU.mult))
                    e.tensor_reduce(worst[:, :], most[:, :], AX_X, ALU.max).then_inc(s_worst, 1)
                    e.wait_ge(s_worst_t, checked + 1)
                    after_own(e.tensor_reduce(worst1[:, 0:1], worst_t[:, :], AX_X, ALU.max))
                    after_own(e.tensor_scalar(worst1[:, 1:2], worst1[:, 0:1], TOLERANCE, None, ALU.is_gt))
                    e.tensor_copy(apart[:, :], worst1[:, 1:2]).then_inc(s_apart, 1)
                    signals += 2 + 4 + 1 + 2
                for k in range(K):
                    after_own(e.tensor_tensor_scan(change[:, k, 1:], decay_t[:, k, 0:L - 1], gap[:, k, 1:],
                                                   0.0, ALU.mult, ALU.add))
                signals += K
                e.tensor_tensor(c_start[:, :, 1:], c_start[:, :, 1:], change[:, :, 1:],
                                ALU.add).then_inc(s_cs, 1)
                e.memset(decay[0:L], 1.0).then_inc(s_fresh, 1)
                e.wait_ge(s_tcs, r + 1)
                after_own(e.tensor_tensor(h_start[:, :, 1:], out_gate_t[:, :, 0:L - 1], tc_start[:, :, 1:],
                                          ALU.mult))
                after_own(e.tensor_copy(h_high[:, :, :], h_start[:, :, :]))
                after_own(e.tensor_tensor(h_low[:, :, :], h_start[:, :, :], h_high[:, :, :].bitcast(F32),
                                          ALU.subtract))
                signals += 3
                e.wait_ge(s_back, r + 1)
                e.tensor_copy(c[0:L].rearrange("c a u -> c (a u)"), back[0:L, :]).then_inc(s_begin, 1)
                e.wait_ge(s_begin, r + 2)
                e.sem_inc(s_own, (FINE_OWN if fine else ROUGH_OWN) - signals)
            all_rounds(e, one_round, s_apart)


_INS = ["x", "src", "dst", "L0_gnn_W1", "L0_gnn_b1", "L0_gnn_W2", "L0_gnn_b2",
        "L0_ffn_W_f", "L0_ffn_W_i", "L0_ffn_W_c", "L0_ffn_W_o",
        "L0_ffn_b_f", "L0_ffn_b_i", "L0_ffn_b_c", "L0_ffn_b_o"]


def kernel(**inputs):
    import numpy as _np
    import concourse.bacc as _bacc
    from concourse import mybir as _mybir
    from concourse.bass_utils import run_bass_kernel_spmd as _run

    nc = _bacc.Bacc("TRN2", target_bir_lowering=False, num_devices=1)
    arrays, args = {}, []
    for name in _INS:
        a = _np.ascontiguousarray(inputs[name])
        arrays[f"in_{name}_dram"] = a
        args.append(nc.dram_tensor(f"in_{name}_dram", a.shape, _mybir.dt.from_np(a.dtype),
                                   kind="ExternalInput").ap())
    shape = tuple(inputs["x"].shape)
    out = nc.dram_tensor("out_0_dram", shape, _mybir.dt.float32, kind="ExternalOutput").ap()
    x, src, dst, W1, b1, W2, b2 = args[:7]
    program(nc, x, src, dst, W1, b1, W2, b2, args[7:11], args[11:15], out)
    r = _run(nc, [arrays], core_ids=[0])
    return r.results[0]["out_0_dram"]
```
